# Optimizing a Trainium2 kernel written in Bass

```python
import numpy as np
import jax
import jax.numpy as jnp

def _softmax(x, axis=-1):
    return jax.nn.softmax(x, axis=axis)

def _gelu(x):
    return jax.nn.gelu(x, approximate=True)

def _silu(x):
    return jax.nn.silu(x)

def _sigmoid(x):
    return jax.nn.sigmoid(x)

def _layernorm(x, axis=-1, eps=1e-05):
    m = jnp.mean(x, axis=axis, keepdims=True)
    v = jnp.var(x, axis=axis, keepdims=True)
    return (x - m) / jnp.sqrt(v + eps)

def _scatter_add(tgt, idx, src, axis=0):
    return tgt.at[idx].add(src)

def _segment_sum(src, seg, n):
    return jax.ops.segment_sum(src, seg, n)
kernel_name = 'mk_dlrm_tower_d1_rec_r8_dc53af'

def setup_inputs(seed: int=0):
    np.random.seed(seed)
    _w = jnp.asarray

    def _rec_inputs():
        import jax
        import jax.numpy as jnp
        _tk = jax.random.key(seed)
        dense_ctx = jax.random.normal(jax.random.fold_in(_tk, 190), (2048, 16), jnp.float32)
        ids = jnp.stack([jax.random.randint(jax.random.fold_in(_tk, 200 + f), (2048,), 0, v, jnp.int32) for f, v in enumerate([125000, 125000, 125000, 1250, 12500, 1250, 12500, 125000, 125000, 1000, 125000, 1250, 12500, 125000, 125000, 125000, 125000, 12500, 12500, 1000, 125000, 12500, 125000, 1000])], axis=1)
        tbl_0 = 0.05 * jax.random.normal(jax.random.fold_in(_tk, 500 + 0), (125000, 16), jnp.float32)
        tbl_1 = 0.05 * jax.random.normal(jax.random.fold_in(_tk, 500 + 1), (125000, 16), jnp.float32)
        tbl_2 = 0.05 * jax.random.normal(jax.random.fold_in(_tk, 500 + 2), (125000, 16), jnp.float32)
        tbl_3 = 0.05 * jax.random.normal(jax.random.fold_in(_tk, 500 + 3), (1250, 16), jnp.float32)
        tbl_4 = 0.05 * jax.random.normal(jax.random.fold_in(_tk, 500 + 4), (12500, 16), jnp.float32)
        tbl_5 = 0.05 * jax.random.normal(jax.random.fold_in(_tk, 500 + 5), (1250, 16), jnp.float32)
        tbl_6 = 0.05 * jax.random.normal(jax.random.fold_in(_tk, 500 + 6), (12500, 16), jnp.float32)
        tbl_7 = 0.05 * jax.random.normal(jax.random.fold_in(_tk, 500 + 7), (125000, 16), jnp.float32)
        tbl_8 = 0.05 * jax.random.normal(jax.random.fold_in(_tk, 500 + 8), (125000, 16), jnp.float32)
        tbl_9 = 0.05 * jax.random.normal(jax.random.fold_in(_tk, 500 + 9), (1000, 16), jnp.float32)
        tbl_10 = 0.05 * jax.random.normal(jax.random.fold_in(_tk, 500 + 10), (125000, 16), jnp.float32)
        tbl_11 = 0.05 * jax.random.normal(jax.random.fold_in(_tk, 500 + 11), (1250, 16), jnp.float32)
        tbl_12 = 0.05 * jax.random.normal(jax.random.fold_in(_tk, 500 + 12), (12500, 16), jnp.float32)
        tbl_13 = 0.05 * jax.random.normal(jax.random.fold_in(_tk, 500 + 13), (125000, 16), jnp.float32)
        tbl_14 = 0.05 * jax.random.normal(jax.random.fold_in(_tk, 500 + 14), (125000, 16), jnp.float32)
        tbl_15 = 0.05 * jax.random.normal(jax.random.fold_in(_tk, 500 + 15), (125000, 16), jnp.float32)
        tbl_16 = 0.05 * jax.random.normal(jax.random.fold_in(_tk, 500 + 16), (125000, 16), jnp.float32)
        tbl_17 = 0.05 * jax.random.normal(jax.random.fold_in(_tk, 500 + 17), (12500, 16), jnp.float32)
        tbl_18 = 0.05 * jax.random.normal(jax.random.fold_in(_tk, 500 + 18), (12500, 16), jnp.float32)
        tbl_19 = 0.05 * jax.random.normal(jax.random.fold_in(_tk, 500 + 19), (1000, 16), jnp.float32)
        tbl_20 = 0.05 * jax.random.normal(jax.random.fold_in(_tk, 500 + 20), (125000, 16), jnp.float32)
        tbl_21 = 0.05 * jax.random.normal(jax.random.fold_in(_tk, 500 + 21), (12500, 16), jnp.float32)
        tbl_22 = 0.05 * jax.random.normal(jax.random.fold_in(_tk, 500 + 22), (125000, 16), jnp.float32)
        tbl_23 = 0.05 * jax.random.normal(jax.random.fold_in(_tk, 500 + 23), (1000, 16), jnp.float32)
        _rk = jax.random.fold_in(_tk, 7)
        W_top1 = 0.0693375 * jax.random.normal(jax.random.fold_in(_tk, 801), (208, 512), jnp.float32)
        W_top2 = 0.0441942 * jax.random.normal(jax.random.fold_in(_tk, 802), (512, 256), jnp.float32)
        W_top3 = 0.0625 * jax.random.normal(jax.random.fold_in(_tk, 803), (256, 1), jnp.float32)
        b_top1 = jnp.zeros((512,), jnp.float32)
        b_top2 = jnp.zeros((256,), jnp.float32)
        return (dense_ctx, ids, tbl_0, tbl_1, tbl_2, tbl_3, tbl_4, tbl_5, tbl_6, tbl_7, tbl_8, tbl_9, tbl_10, tbl_11, tbl_12, tbl_13, tbl_14, tbl_15, tbl_16, tbl_17, tbl_18, tbl_19, tbl_20, tbl_21, tbl_22, tbl_23, W_top1, b_top1, W_top2, b_top2, W_top3)
    dense_ctx, ids, tbl_0, tbl_1, tbl_2, tbl_3, tbl_4, tbl_5, tbl_6, tbl_7, tbl_8, tbl_9, tbl_10, tbl_11, tbl_12, tbl_13, tbl_14, tbl_15, tbl_16, tbl_17, tbl_18, tbl_19, tbl_20, tbl_21, tbl_22, tbl_23, W_top1, b_top1, W_top2, b_top2, W_top3 = _rec_inputs()

    def _L0_rec_setup():
        import jax, jax.numpy as jnp
        import numpy as np
        B, F, D = (512, 24, 16)
        LAYER_SIZES = [64, 64, 64]

        def _cin_forward(X0, Ws):
            F_ = X0.shape[1]
            Xk = X0
            outs = []
            for W in Ws:
                H_prev = Xk.shape[1]
                Wr = W.reshape(F_, H_prev, W.shape[1])
                Xk = jnp.einsum('bfd,bhd,fho->bod', X0, Xk, Wr)
                outs.append(Xk.sum(axis=2))
            return jnp.concatenate(outs, axis=1)
        key = jax.random.key(seed)
        k0, k1, k2, k3 = jax.random.split(key, 4)
        X0 = jax.random.normal(k0, (B, F, D), dtype=jnp.float32)
        prev = F
        Ws = []
        for k, h in zip((k1, k2, k3), LAYER_SIZES):
            Ws.append(jax.random.normal(k, (prev * F, h), dtype=jnp.float32) * 0.01)
            prev = h
        return {'X0': X0, 'W0': Ws[0], 'W1': Ws[1], 'W2': Ws[2]}
    _L0_rec_all = _L0_rec_setup()
    _L0_rec_in = {k: v for k, v in _L0_rec_all.items() if k in ('W0', 'W1', 'W2')}
    del _L0_rec_all
    return {'dense_ctx': dense_ctx, 'ids': ids, 'tbl_0': tbl_0, 'tbl_1': tbl_1, 'tbl_2': tbl_2, 'tbl_3': tbl_3, 'tbl_4': tbl_4, 'tbl_5': tbl_5, 'tbl_6': tbl_6, 'tbl_7': tbl_7, 'tbl_8': tbl_8, 'tbl_9': tbl_9, 'tbl_10': tbl_10, 'tbl_11': tbl_11, 'tbl_12': tbl_12, 'tbl_13': tbl_13, 'tbl_14': tbl_14, 'tbl_15': tbl_15, 'tbl_16': tbl_16, 'tbl_17': tbl_17, 'tbl_18': tbl_18, 'tbl_19': tbl_19, 'tbl_20': tbl_20, 'tbl_21': tbl_21, 'tbl_22': tbl_22, 'tbl_23': tbl_23, 'W_top1': W_top1, 'b_top1': b_top1, 'W_top2': W_top2, 'b_top2': b_top2, 'W_top3': W_top3, 'L0_rec_W0': _L0_rec_in['W0'], 'L0_rec_W1': _L0_rec_in['W1'], 'L0_rec_W2': _L0_rec_in['W2']}

def reference(dense_ctx, ids, tbl_0, tbl_1, tbl_2, tbl_3, tbl_4, tbl_5, tbl_6, tbl_7, tbl_8, tbl_9, tbl_10, tbl_11, tbl_12, tbl_13, tbl_14, tbl_15, tbl_16, tbl_17, tbl_18, tbl_19, tbl_20, tbl_21, tbl_22, tbl_23, W_top1, b_top1, W_top2, b_top2, W_top3, L0_rec_W0, L0_rec_W1, L0_rec_W2):
    import jax
    import jax.numpy as jnp

    def _L0_rec_ref(X0, W0, W1, W2):
        import jax, jax.numpy as jnp
        import numpy as np
        B, F, D = (512, 24, 16)
        LAYER_SIZES = [64, 64, 64]

        def _cin_forward(X0, Ws):
            F_ = X0.shape[1]
            Xk = X0
            outs = []
            for W in Ws:
                H_prev = Xk.shape[1]
                Wr = W.reshape(F_, H_prev, W.shape[1])
                Xk = jnp.einsum('bfd,bhd,fho->bod', X0, Xk, Wr)
                outs.append(Xk.sum(axis=2))
            return jnp.concatenate(outs, axis=1)
        return _cin_forward(X0, (W0, W1, W2))
    e = jnp.stack([tbl_0[ids[:, 0]], tbl_1[ids[:, 1]], tbl_2[ids[:, 2]], tbl_3[ids[:, 3]], tbl_4[ids[:, 4]], tbl_5[ids[:, 5]], tbl_6[ids[:, 6]], tbl_7[ids[:, 7]], tbl_8[ids[:, 8]], tbl_9[ids[:, 9]], tbl_10[ids[:, 10]], tbl_11[ids[:, 11]], tbl_12[ids[:, 12]], tbl_13[ids[:, 13]], tbl_14[ids[:, 14]], tbl_15[ids[:, 15]], tbl_16[ids[:, 16]], tbl_17[ids[:, 17]], tbl_18[ids[:, 18]], tbl_19[ids[:, 19]], tbl_20[ids[:, 20]], tbl_21[ids[:, 21]], tbl_22[ids[:, 22]], tbl_23[ids[:, 23]]], axis=1)
    z = _L0_rec_ref(e, L0_rec_W0, L0_rec_W1, L0_rec_W2)
    z = z.reshape(z.shape[0], -1)
    h = jnp.concatenate([z, dense_ctx], axis=1)
    h = jnp.maximum(h @ W_top1 + b_top1, 0.0)
    h = jnp.maximum(h @ W_top2 + b_top2, 0.0)
    y = h @ W_top3
    return y

_drawn_inputs = setup_inputs


def setup_inputs(seed=0):
    import zlib

    import numpy as np

    out = dict(_drawn_inputs(seed))
    spreads = {'b_top1': (0.0, 0.1), 'b_top2': (0.0, 0.1)}
    factors = {'tbl_0': 8.0,
     'tbl_1': 8.0,
     'tbl_2': 8.0,
     'tbl_3': 8.0,
     'tbl_4': 8.0,
     'tbl_5': 8.0,
     'tbl_6': 8.0,
     'tbl_7': 8.0,
     'tbl_8': 8.0,
     'tbl_9': 8.0,
     'tbl_10': 8.0,
     'tbl_11': 8.0,
     'tbl_12': 8.0,
     'tbl_13': 8.0,
     'tbl_14': 8.0,
     'tbl_15': 8.0,
     'tbl_16': 8.0,
     'tbl_17': 8.0,
     'tbl_18': 8.0,
     'tbl_19': 8.0,
     'tbl_20': 8.0,
     'tbl_21': 8.0,
     'tbl_22': 8.0,
     'tbl_23': 8.0,
     'L0_rec_W0': 8.0,
     'L0_rec_W1': 8.0,
     'L0_rec_W2': 8.0}
    for name, (base, spread) in spreads.items():
        noise = np.random.default_rng([zlib.crc32(name.encode()), seed]).standard_normal(out[name].shape)
        drawn = base * np.exp(spread * noise) if base else spread * noise
        out[name] = jnp.asarray(drawn.astype(out[name].dtype))
    for name, factor in factors.items():
        out[name] = (out[name] * factor).astype(out[name].dtype)
    return out
```

```python
from contextlib import ExitStack

import concourse.bass as bass
from concourse import mybir

F32 = mybir.dt.float32
BF16 = mybir.dt.bfloat16
I32 = mybir.dt.int32
U32 = mybir.dt.uint32
ALU = mybir.AluOpType
ACT = mybir.ActivationFunctionType
AX = mybir.AxisListType

B, F, D, H, DENSE = 2048, 24, 16, 64, 16
T1, T2 = 512, 256
TB = 128
TILES = B // TB
PAIRS = 2 * TILES
PB = TB // 2
COLS = PB * D
BLK = COLS // 2
BB = BLK // D
CH = COLS // 128
CB = 128 // D
PARTS = 3
KX = PARTS * F
SH = F // 2 + 1
SHC = 5
L0_ROWS = [SHC * F, SHC * F, 2 * F + F // 2]
FC = F // 2
GF = FC + 1
FC_STEPS = FC // 2


def spread_schedule():
    a = [("two", 0, i) for i in range(FC_STEPS)]
    b = [("two", 1, i) for i in range(FC_STEPS)]
    s = [("one", i) for i in range(3)]
    full = [("rep",), a[0], a[1], s[0], a[2], a[3], s[1], a[4], a[5], s[2]] + b
    return full, [("rep",)] + s, a + b


FULL, FIRST, LAST = spread_schedule()
PER_SLOT = len(FULL) - 1
NZ = 4
PICKS = [FC * 128, 4 * SHC * F, F, 128]


class Slot:

    def __init__(self, q, r, number=None):
        self.q, self.r = q, r
        n = number
        self.one = n is None or n < PAIRS
        self.two = n is None or 1 <= n <= PAIRS
        self.gram = n is None or 2 <= n
        self.steps = FULL if self.one and self.two else FIRST if self.one else LAST if self.two else []
        self.split = n != 0 and (r % 2 == 0 or n == 1) and (n is None or n <= PAIRS - 4)
        self.turn = r % 2 == 1 and (n is None or n <= PAIRS - 3)
        self.number = n
        self.done = 0 if n == 0 else q * PER_SLOT - (PER_SLOT - 3)

    def nth(self, pos):
        return self.done + (pos + 1 if self.steps is LAST else pos)

    def nth_of(self, *step):
        return self.nth(self.steps.index(step))


def slots(engine):
    yield Slot(0, 0, 0)
    yield Slot(1, 1, 1)
    with engine.Fori(0, (PAIRS - 4) // 4) as i:
        for j in range(4):
            yield Slot(i * 4 + (2 + j), (2 + j) % 4)
    for n in range(PAIRS - 2, PAIRS + 2):
        yield Slot(n, n % 4, n)


def tower(nc, x):
    with ExitStack() as ctx:
        def sb(name, shape, dt=F32):
            return ctx.enter_context(nc.sbuf_tensor(name, shape, dt))

        def sem(name):
            return ctx.enter_context(nc.semaphore(name))

        w0a = sb("w0a", [SHC * F, 3, H])
        w0b = sb("w0b", [SHC * F, 3, H])
        w1 = sb("w1", [128, FC, H])
        w2 = sb("w2", [128, FC, H])
        wt1a = sb("wt1a", [2 * H, T1])
        wt1b = sb("wt1b", [H + DENSE, T1])
        wt2 = sb("wt2", [128, T1 // 128, T2])
        wt3 = sb("wt3", [128, T2 // 128])
        bt1 = sb("bt1", [128, T1 // 128])
        bt2 = sb("bt2", [128, T2 // 128])
        picks = sb("picks", [128, sum(PICKS)], BF16)
        at = [sum(PICKS[:n]) for n in range(len(PICKS) + 1)]
        spread_two = picks[0:KX, at[0]:at[1]].rearrange("k (c m) -> k c m", c=FC)
        spread_one = picks[0:KX, at[1]:at[2]].rearrange("k (c m) -> k c m", c=4)
        collect = picks[0:KX, at[2]:at[3]]
        ident = picks[:, at[3]:at[4]]
        fold = sb("fold", [128, H])
        own_row = sb("own_row", [128, CB])
        idx = sb("idx", [128, 2, F], I32)
        emb = sb("emb", [TB, 2, F, D])
        rest = sb("rest", [TB, F, D])
        parts = sb("parts", [TB, D, PARTS, F], BF16)
        x0s = sb("x0s", [KX, 2, TB * D], BF16)
        rep = sb("rep", [SHC * F, COLS])
        prod = sb("prod", [128, NZ, 2, BLK])
        x1 = sb("x1", [128, 2, COLS])
        x2 = sb("x2", [128, COLS])
        x2t = sb("x2t", [128, CH, H])
        x0t = sb("x0t", [128, 2, CH, F])
        diag = sb("diag", [128, 2, CH, CB, 1 + F])
        sum1 = sb("sum1", [128, PAIRS * BB])
        gram = sb("gram", [128, GF, B])
        z12 = gram[:, 0, :]
        z0d = prod[:, 2:4].rearrange("p a b c -> p (a b c)")[0:H + DENSE]
        h1 = [x1[:].rearrange("p a c -> p (a c)"),
              diag[:].rearrange("p a c b f -> p (a c b f)")[:, 0:4 * 512]]
        h2 = [x2[:, :], sb("h2b", [128, 1024])[:, :]] + [prod[:, n].rearrange("p b c -> p (b c)") for n in range(2)]
        y = sb("y", [128, 512])

        ps = [ctx.enter_context(nc.psum_tensor(f"spread{i}", [128, 2, BLK], F32)) for i in range(2)]
        acc1 = ctx.enter_context(nc.psum_tensor("acc1", [128, BLK], F32))
        acc2 = ctx.enter_context(nc.psum_tensor("acc2", [128, BLK], F32))
        misc = [ctx.enter_context(nc.psum_tensor(f"misc{i}", [128, BLK], F32)) for i in range(2)]

        weights_in = sem("weights_in")
        ids_in = [sem(f"ids_in{i}") for i in range(2)]
        gathered = [sem(f"gathered{i}") for i in range(2)]
        dense_in = sem("dense_in")
        stored = sem("stored")
        w0_zeroed, w0_summed = sem("w0_zeroed"), sem("w0_summed")
        diag_ones, picks_done = sem("diag_ones"), sem("picks_done")
        hi_done, rest_done, mid_done, lo_done = sem("hi_done"), sem("rest_done"), sem("mid_done"), sem("lo_done")
        turned, turn_copied = sem("turned"), sem("turn_copied")
        rep_spread, rep_copied = sem("rep_spread"), sem("rep_copied")
        spread = sem("spread")
        multiplied = sem("multiplied")
        contracted = sem("contracted")
        acc1_summed, x1_copied, x2_copied = sem("acc1_summed"), sem("x1_copied"), sem("x2_copied")
        x0t_ready, x0t_copied = sem("x0t_ready"), sem("x0t_copied")
        diag_done = sem("diag_done")
        x2t_ready, x2t_copied = sem("x2t_ready"), sem("x2t_copied")
        gram_ready, gram_copied = sem("gram_ready"), sem("gram_copied")
        out2_ready, z_copied = sem("out2_ready"), sem("z_copied")
        mm1_ready, h1_done = sem("mm1_ready"), sem("h1_done")
        mm2_ready, h2_done = sem("mm2_ready"), sem("h2_done")
        mm3_ready, y_done = sem("mm3_ready"), sem("y_done")

        picks_f32 = prod[:].rearrange("p a b c -> p (a b c)")[:, 0:sum(PICKS)]
        loads = [
            (picks_f32, x["picks"]), (fold[:, :], x["fold"]), (own_row[:, :], x["own_row"]),
        ]
        w0s = x["w0_lower"].shape[0]
        loads += [(w0a[0:SHC * F, c, :], x["w0_upper"][c * SHC * F:(c + 1) * SHC * F, :]) for c in range(2)]
        loads += [(w0a[0:L0_ROWS[2], 2, :], x["w0_upper"][2 * SHC * F:w0s + F, :])]
        loads += [(w0b[F:SHC * F, 0, :], x["w0_lower"][0:(SHC - 1) * F, :]),
                  (w0b[0:SHC * F, 1, :], x["w0_lower"][(SHC - 1) * F:(2 * SHC - 1) * F, :]),
                  (w0b[0:L0_ROWS[2], 2, :], x["w0_lower"][(2 * SHC - 1) * F:w0s, :])]
        loads += [(w1[:, :, :], x["w1"].rearrange("(c p) o -> p c o", p=128))]
        loads += [(w2[:, :, :], x["w2"].rearrange("(c p) o -> p c o", p=128))]
        loads += [(wt1a[:, :], x["wt1"][H:3 * H, :]), (wt1b[0:H, :], x["wt1"][0:H, :]),
                  (wt1b[H:H + DENSE, :], x["wt1"][3 * H:3 * H + DENSE, :]),
                  (wt2[:, :, :], x["wt2"].rearrange("(c p) n -> p c n", p=128)),
                  (wt3[:, :], x["wt3"]), (bt1[:, :], x["bt1"]), (bt2[:, :], x["bt2"])]
        ALL_LOADED = 16 * len(loads)

        def gathers_of(tile):
            return 16 * F * (tile // 2 + 1)

        block = ctx.enter_context(nc.Block())

        @block.sync
        def _(sp):
            for t in range(2):
                sp.dma_start(idx[:, t, :], x["ids"][t * TB:(t + 1) * TB, :]).then_inc(ids_in[t], 16)
            for dst, src in loads:
                sp.dma_start(dst, src).then_inc(weights_in, 16)
            with sp.Fori(0, TILES // 2 - 1) as i:
                for s in range(2):
                    sp.wait_ge(gathered[s], i * (16 * F) + 16 * F)
                    sp.dma_start(idx[:, s, :], x["ids"][bass.ds(i * (2 * TB) + (2 + s) * TB, TB), :])\
                      .then_inc(ids_in[s], 16)
            sp.wait_ge(contracted, PER_SLOT * (PAIRS - 1) + 3 + len(LAST))
            sp.dma_start(z0d[H:H + DENSE, :], x["dense_t"]).then_inc(dense_in, 16)
            sp.wait_ge(y_done, 1)
            sp.dma_start(x["out"].rearrange("(n b) a -> n (b a)", n=4), y[0:128:32, :]).then_inc(stored, 16)
            sp.wait_ge(stored, 16)

        @block.gpsimd
        def _(pool):
            def gather(s, first, last):
                for f in range(first, last):
                    nc.gpsimd.indirect_dma_start(
                        out=emb[:, s, f, :], out_offset=None, in_=x["tables"][f],
                        in_offset=bass.IndirectOffsetOnAxis(ap=idx[:, s, f:f + 1].bitcast(U32), axis=0),
                    ).then_inc(gathered[s], 16)

            def diagonals(slot):
                q, s = slot.q, (slot.r - 1) % 2
                pool.wait_ge(x0t_copied, q)
                if slot.gram:
                    pool.wait_ge(gram_ready, q * 2 - 3)
                nc.gpsimd.tensor_tensor(
                    diag[:, s, :, :, 1:1 + F], x0t[:, s, :, :].unsqueeze(2).broadcast_to([128, CH, CB, F]),
                    own_row[:, :].unsqueeze(1).unsqueeze(3).broadcast_to([128, CH, CB, F]), ALU.mult,
                ).then_inc(diag_done, 1)

            for s in range(2):
                pool.wait_ge(ids_in[s], 16)
                gather(s, 0, F)
            pool.wait_ge(weights_in, ALL_LOADED)
            for s in range(2):
                nc.gpsimd.tensor_copy(diag[:, s, :, :, 0],
                                      own_row[:, :].unsqueeze(1).broadcast_to([128, CH, CB])).then_inc(diag_ones, 1)

            def slot_work(slot, fetch):
                s, half = slot.r // 2, slot.r % 2
                if fetch and half == 0:
                    if slot.number is None:
                        ids_value, rest_value = fetch
                    else:
                        t = slot.q // 2
                        ids_value, rest_value = 16 * ((t + 2) // 2 + 1), t + 1
                    pool.wait_ge(ids_in[s], ids_value)
                    pool.wait_ge(rest_done, rest_value)
                if slot.two:
                    diagonals(slot)
                if fetch:
                    gather(s, half * F // 2, (half + 1) * F // 2)

            slot_work(Slot(0, 0, 0), True)
            slot_work(Slot(1, 1, 1), True)
            with pool.Fori(0, (PAIRS - 8) // 4) as i:
                for j in range(4):
                    t0 = 1 + j // 2
                    slot_work(Slot(i * 4 + (2 + j), (2 + j) % 4),
                              (i * 16 + 16 * ((t0 + 2) // 2 + 1), i * 2 + (t0 + 1)))
            for n in range(PAIRS - 6, PAIRS + 1):
                slot_work(Slot(n, n % 4, n), n < PAIRS - 4)

        @block.scalar
        def _(act):
            copy = ACT.Copy

            def split_hi(s, gathered_value, turned_value):
                act.wait_ge(gathered[s], gathered_value)
                if turned_value is not None:
                    act.wait_ge(turned, turned_value)
                nc.scalar.activation(parts[:, :, 0, :].rearrange("p d f -> p f d"), emb[:, s, :, :], copy)\
                    .then_inc(hi_done, 1)

            def split_mid(rest_value):
                act.wait_ge(rest_done, rest_value)
                nc.scalar.activation(parts[:, :, 1, :].rearrange("p d f -> p f d"), rest[:, :, :], copy)\
                    .then_inc(mid_done, 1)

            def copy_turned(s, g, value):
                act.wait_ge(turned, value)
                nc.scalar.activation(
                    x0s[:, s, :].rearrange("k (b d) -> k d b", d=D)[:, g * 8:g * 8 + 8, :],
                    misc[g][0:KX, :].bitcast(BF16).rearrange("k (d b) -> k d b", b=TB), copy,
                ).then_inc(turn_copied, 1)

            def copy_rep(q):
                act.wait_ge(rep_spread, q + 1)
                nc.scalar.activation(rep[:, :], ps[0][0:SHC * F].rearrange("p a c -> p (a c)"), copy)\
                    .then_inc(rep_copied, 1)

            def copy_x1(slot):
                act.wait_ge(acc1_summed, slot.q + 1)
                for blk in range(2):
                    for half in range(2):
                        c = nc.scalar.activation(x1[H * half:H * half + H, slot.r % 2, blk * BLK:(blk + 1) * BLK],
                                                 acc1[H * blk:H * blk + H, :], copy)
                c.then_inc(x1_copied, 1)

            def copy_x2(slot, blk):
                act.wait_ge(contracted, slot.nth_of("two", blk, FC_STEPS - 1))
                nc.scalar.activation(x2[:, blk * BLK:(blk + 1) * BLK], acc2[:, :], copy).then_inc(x2_copied, 1)

            def copy_gram(slot, part):
                q = slot.q
                act.wait_ge(gram_ready, q * 2 + (part - 3))
                cols = CH // 2 * CB
                first = (q - 2) * PB + part * cols
                nc.scalar.activation(
                    gram[:, :, bass.ds(first, cols)].rearrange("p f (c b) -> p c b f", b=CB),
                    misc[part][:, 0:cols * GF].rearrange("p (c b f) -> p c b f", b=CB, f=GF), copy,
                ).then_inc(gram_copied, 1)

            def slot_work(slot, gathered_value):
                q, r = slot.q, slot.r
                tile_s = (1 if slot.number == 1 else r // 2 + 1) % 2
                if slot.split:
                    T = 1 if slot.number == 1 else None
                    split_hi(tile_s, gathered_value, 2 if T else q + 2)
                if slot.two:
                    act.wait_ge(x0t_ready, q)
                    if slot.number != 1:
                        act.wait_ge(diag_done, q - 1)
                    nc.scalar.activation(x0t[:, (r - 1) % 2, :, :], misc[0][:, 0:CH * F].rearrange("p (c f) -> p c f", f=F),
                                         copy).then_inc(x0t_copied, 1)
                if slot.gram:
                    act.wait_ge(x2t_ready, q - 1)
                    nc.scalar.activation(x2t[:, :, :], misc[1][:, :].rearrange("p (c o) -> p c o", o=H), copy)\
                        .then_inc(x2t_copied, 1)
                    copy_gram(slot, 0)
                if slot.split:
                    split_mid(2 if slot.number == 1 else T_of(slot))
                if slot.gram:
                    copy_gram(slot, 1)
                if slot.two:
                    copy_x2(slot, 0)
                if slot.turn:
                    copy_turned(((r + 1) // 2) % 2, 0, q + 2)
                    copy_turned(((r + 1) // 2) % 2, 1, q + 3)
                if slot.one:
                    copy_x1(slot)
                if slot.number is None or slot.number + 1 < PAIRS:
                    copy_rep(q + 1)
                if slot.two:
                    copy_x2(slot, 1)

            def T_of(slot):
                return slot.half + 2 if slot.half is not None else slot.q // 2 + 2

            act.wait_ge(weights_in, ALL_LOADED)
            nc.scalar.activation(picks[:, :], picks_f32, copy).then_inc(picks_done, 1)
            split_hi(0, gathers_of(0), None)
            split_mid(1)
            copy_turned(0, 0, 1)
            copy_turned(0, 1, 2)
            copy_rep(0)
            for n in (0, 1):
                slot = Slot(n, n, n)
                slot.half = None
                slot_work(slot, gathers_of(1))
            with act.Fori(0, (PAIRS - 4) // 4) as i:
                for j in range(4):
                    slot = Slot(i * 4 + (2 + j), (2 + j) % 4)
                    slot.half = i * 2 + (1 + j // 2)
                    slot_work(slot, i * (16 * F) + 16 * F * ((2 + j // 2) // 2 + 1))
            for n in range(PAIRS - 2, PAIRS + 2):
                slot = Slot(n, n % 4, n)
                slot.half = None
                slot_work(slot, None)

            act.wait_ge(contracted, PER_SLOT * (PAIRS - 1) + 3 + len(LAST))
            z0v = z0d[0:H, :].rearrange("p (q k b) -> p k q b", k=2, b=BB)
            for k in range(2):
                last = nc.scalar.activation(z0v[:, k], sum1[H * k:H * k + H, :].rearrange("p (q b) -> p q b", b=BB), copy)
            last.then_inc(z_copied, 1)
            act.wait_ge(gram_copied, 2 * PAIRS)
            for n in range(2):
                act.wait_ge(out2_ready, n + 1)
                for k in range(2):
                    last = nc.scalar.activation(z12[H:2 * H, (2 * n + k) * 512:(2 * n + k + 1) * 512],
                                                misc[n][H * k:H * k + H, :], copy)
                last.then_inc(z_copied, 1)
            act.wait_ge(weights_in, ALL_LOADED)
            for nb in range(4):
                for m in range(T1 // 128):
                    n = nb * (T1 // 128) + m
                    act.wait_ge(mm1_ready, n + 1)
                    if m == 0 and nb >= 2:
                        act.wait_ge(mm2_ready, 2 * (nb - 1))
                    nc.scalar.activation(h1[nb % 2][:, m * 512:(m + 1) * 512], ps[n % 2][:, 0, :], ACT.Relu,
                                         bias=bt1[:, m:m + 1]).then_inc(h1_done, 1)

        @block.vector
        def _(dve):
            def split_rest(s, hi_value):
                dve.wait_ge(hi_done, hi_value)
                nc.vector.tensor_tensor(rest[:, :, :], emb[:, s, :, :], parts[:, :, 0, :].rearrange("p d f -> p f d"),
                                        ALU.subtract).then_inc(rest_done, 1)

            def split_lo(mid_value):
                dve.wait_ge(mid_done, mid_value)
                nc.vector.tensor_tensor(parts[:, :, 2, :].rearrange("p d f -> p f d"), rest[:, :, :],
                                        parts[:, :, 1, :].rearrange("p d f -> p f d"), ALU.subtract)\
                    .then_inc(lo_done, 1)

            def product(slot, pos, step):
                nth = slot.nth(pos)
                dve.wait_ge(spread, nth)
                back = 3 if pos <= 3 and slot.steps is FULL else NZ
                if slot.number is None or nth - back > 0:
                    dve.wait_ge(contracted, nth - back)
                src, dst = ps[pos % 2], prod[:, pos % NZ]
                if step[0] == "one":
                    if step[1] == 0:
                        dve.wait_ge(rep_copied, slot.q + 1)
                    rows = L0_ROWS[step[1]]
                    nc.vector.tensor_tensor(dst[0:rows].rearrange("p a c -> p (a c)"), src[0:rows].rearrange("p a c -> p (a c)"),
                                            rep[0:rows, :], ALU.mult).then_inc(multiplied, 1)
                else:
                    _, blk, i = step
                    if i == 0 and blk == 0:
                        dve.wait_ge(x1_copied, slot.q)
                    xx = x1[:, (slot.r - 1) % 2, blk * BLK:(blk + 1) * BLK].unsqueeze(1).broadcast_to([128, 2, BLK])
                    nc.vector.tensor_tensor(dst, src[:, :, :], xx, ALU.mult).then_inc(multiplied, 1)

            def sum_x1(slot):
                dve.wait_ge(contracted, slot.nth_of("one", 2))
                nc.vector.tensor_reduce(sum1[:, bass.ds(slot.q * BB, BB)], acc1[:, :].rearrange("p (b d) -> p b d", d=D),
                                        AX.X, ALU.add).then_inc(acc1_summed, 1)

            def slot_work(slot):
                T = None
                for pos, step in enumerate(slot.steps):
                    product(slot, pos, step) if step[0] != "rep" else None
                    if slot.split and pos == 3:
                        split_rest(slot.split_s, slot.split_value)
                    if slot.split and pos == 7:
                        split_lo(slot.split_value)
                    if slot.one and pos == (12 if slot.steps is FULL else 3):
                        sum_x1(slot)

            nc.vector.memset(w0b[0:F, 0, :], 0.0).then_inc(w0_zeroed, 1)
            dve.wait_ge(weights_in, ALL_LOADED)
            dve.wait_ge(w0_zeroed, 1)
            nc.vector.tensor_tensor(w0a[:, 0:2, :], w0a[:, 0:2, :], w0b[:, 0:2, :], ALU.add).then_inc(w0_summed, 1)
            nc.vector.tensor_tensor(w0a[0:L0_ROWS[2], 2, :], w0a[0:L0_ROWS[2], 2, :], w0b[0:L0_ROWS[2], 2, :], ALU.add)\
                .then_inc(w0_summed, 1)
            split_rest(0, 1)
            split_lo(1)
            for n in (0, 1):
                slot = Slot(n, n, n)
                slot.split_s, slot.split_value = 1, 2
                slot_work(slot)
            with dve.Fori(0, (PAIRS - 4) // 4) as i:
                for j in range(4):
                    slot = Slot(i * 4 + (2 + j), (2 + j) % 4)
                    slot.split_s = (j // 2) % 2
                    slot.split_value = i * 2 + (3 + j // 2)
                    slot_work(slot)
            for n in range(PAIRS - 2, PAIRS + 2):
                slot_work(Slot(n, n % 4, n))

            for nb in range(4):
                for m in range(2):
                    dve.wait_ge(mm2_ready, 2 * nb + m + 1)
                    nc.vector.tensor_scalar(h2[nb][:, m * 512:(m + 1) * 512], misc[m][:, :], bt2[:, m:m + 1], 0.0,
                                            ALU.add, ALU.max).then_inc(h2_done, 1)
            dve.wait_ge(mm3_ready, 1)
            nc.vector.tensor_copy(y[:, :], acc1[:, :]).then_inc(y_done, 1)

        @block.tensor
        def _(pe):
            def turn(s_group, value):
                g = s_group
                if g == 0:
                    pe.wait_ge(lo_done, value)
                dst = misc[g][0:KX, :].bitcast(BF16)
                for k in range(8):
                    m = nc.tensor.transpose(dst[:, k * TB:(k + 1) * TB],
                                            parts[:, g * 8 + k, :, :].rearrange("b p f -> b (p f)"), ident[:, :])
                m.then_inc(turned, 1)

            def spread_into(slot, pos):
                step = slot.steps[pos]
                if step[0] == "two":
                    _, blk, i = step
                    r = (slot.r - 1) % 4
                    base = (r % 2) * COLS + blk * BLK
                    for k in range(2):
                        m = nc.tensor.matmul(ps[pos % 2][:, k, :], spread_two[:, 2 * i + k, :],
                                             x0s[:, r // 2, base:base + BLK], start=True, stop=True)
                    m.then_inc(spread, 1)
                    return
                c = 0 if step[0] == "rep" else step[1] + 1
                rows = SHC * F if step[0] == "rep" else L0_ROWS[step[1]]
                base = (slot.r % 2) * COLS
                for blk in range(2):
                    m = nc.tensor.matmul(ps[pos % 2][0:rows, blk, :], spread_one[:, c, 0:rows],
                                         x0s[:, slot.r // 2, base + blk * BLK:base + (blk + 1) * BLK], start=True, stop=True)
                m.then_inc(rep_spread if step[0] == "rep" else spread, 1)

            def contract(slot, pos):
                step, z = slot.steps[pos], prod[:, pos % NZ]
                if step[0] == "one":
                    c, rows = step[1], L0_ROWS[step[1]]
                    if c == 0 and (slot.number is None or slot.number > 0):
                        pe.wait_ge(x1_copied, slot.q)
                    for blk in range(2):
                        m = nc.tensor.matmul(acc1[H * blk:H * blk + H, :], w0a[0:rows, c, :], z[0:rows, blk, :],
                                             start=c == 0, stop=c == 2)
                    m.then_inc(contracted, 1)
                    return
                _, blk, i = step
                if i == 0 and (blk == 1 or slot.number != 1):
                    pe.wait_ge(x2_copied, slot.q * 2 + (blk - 2))
                for k in range(2):
                    m = nc.tensor.matmul(acc2[H * k:H * k + H, :], w1[:, 2 * i + k, :], z[:, k, :],
                                         start=i == 0, stop=i == FC_STEPS - 1)
                m.then_inc(contracted, 1)

            def gram_before(slot):
                return slot.number >= PAIRS if slot.number is not None and slot.r % 2 == 0 else slot.r % 2 == 1 and slot.number != 1

            def collect_x0t(slot):
                r = (slot.r - 1) % 4
                if gram_before(slot):
                    pe.wait_ge(gram_copied, slot.q * 2 - 5)
                for c in range(CH):
                    base = (r % 2) * COLS + c * 128
                    m = nc.tensor.matmul(misc[0][:, c * F:(c + 1) * F], x0s[:, r // 2, base:base + 128], collect[:, :],
                                         start=True, stop=True)
                m.then_inc(x0t_ready, 1)

            def turn_x2(slot, blk):
                q = slot.q
                pe.wait_ge(x2_copied, q * 2 + (blk - 3))
                if blk == 0 and gram_before(slot):
                    pe.wait_ge(gram_copied, q * 2 - 4)
                half = CH // 2
                for c in range(blk * half, (blk + 1) * half):
                    m = nc.tensor.matmul(misc[1][:, c * H:(c + 1) * H], x2[:, c * 128:(c + 1) * 128], fold[:, :],
                                         start=True, stop=True)
                if blk == 1:
                    m.then_inc(x2t_ready, 1)

            def gram_of(slot, part):
                q, s = slot.q, slot.r % 2
                if part == 0:
                    pe.wait_ge(x2t_copied, q - 1)
                    pe.wait_ge(diag_done, q - 1)
                    if slot.two:
                        pe.wait_ge(x0t_copied, q)
                    else:
                        pe.wait_ge(gram_copied, q * 2 - 5)
                width = CB * GF
                for c in range(CH // 2):
                    for odd in range(2):
                        ch = part * (CH // 2) + c
                        m = nc.tensor.matmul(misc[part][H * odd:H * odd + H, c * width:(c + 1) * width], x2t[:, ch, :],
                                             diag[:, s, ch, :, FC * odd:FC * odd + GF], start=True, stop=True)
                m.then_inc(gram_ready, 1)

            def slot_work(slot, after, lo_value):
                q = slot.q
                count = len(slot.steps)
                for pos in range(max(count, 1)):
                    if slot.steps:
                        step = slot.steps[pos]
                        if step[0] == "rep":
                            pe.wait_ge(rep_copied, q + 1)
                        else:
                            pe.wait_ge(multiplied, slot.nth(pos))
                        if pos + 2 < count:
                            spread_into(slot, pos + 2)
                        elif after.steps:
                            if pos + 2 == count and slot.turn:
                                pe.wait_ge(turn_copied, q + 3)
                            spread_into(after, pos + 2 - count)
                        if step[0] != "rep":
                            contract(slot, pos)
                    if pos == 0 and slot.two:
                        collect_x0t(slot)
                    if pos == 0 and slot.gram:
                        turn_x2(slot, 0)
                    if slot.gram and pos == (2 if count else 0):
                        turn_x2(slot, 1)
                    if slot.gram and pos == (0 if not count else 5 if slot.one else 3):
                        gram_of(slot, 0)
                    if slot.gram and pos == (0 if not count else 7 if slot.one else 4):
                        gram_of(slot, 1)
                    if slot.turn and pos == 9:
                        if slot.gram:
                            pe.wait_ge(gram_copied, q * 2 - 3)
                        else:
                            pe.wait_ge(x0t_copied, q)
                        turn(0, lo_value)
                    if slot.turn and pos == 10:
                        if slot.gram:
                            pe.wait_ge(gram_copied, q * 2 - 2)
                        turn(1, None)

            pe.wait_ge(weights_in, ALL_LOADED)
            pe.wait_ge(picks_done, 1)
            turn(0, 1)
            turn(1, None)
            pe.wait_ge(turn_copied, 2)
            first, second = Slot(0, 0, 0), Slot(1, 1, 1)
            spread_into(first, 0)
            spread_into(first, 1)
            pe.wait_ge(w0_summed, 2)
            slot_work(first, second, None)
            slot_work(second, Slot(2, 2, 2), 2)
            with pe.Fori(0, (PAIRS - 4) // 4) as i:
                for j in range(4):
                    slot_work(Slot(i * 4 + (2 + j), (2 + j) % 4), Slot(i * 4 + (3 + j), (3 + j) % 4),
                              i * 2 + ((3 + j) // 2 + 1))
            for n in range(PAIRS - 2, PAIRS + 2):
                slot_work(Slot(n, n % 4, n), Slot(n + 1, (n + 1) % 4, n + 1), None)

            pe.wait_ge(gram_copied, 2 * PAIRS)
            for n in range(2):
                for c in range(FC):
                    for k in range(2):
                        m = nc.tensor.matmul(misc[n][H * k:H * k + H, :], w2[:, c, :],
                                             gram[:, 1 + c, (2 * n + k) * 512:(2 * n + k + 1) * 512],
                                             start=c == 0, stop=c == FC - 1)
                m.then_inc(out2_ready, 1)
            pe.wait_ge(dense_in, 16)

            def layer1(nb):
                pe.wait_ge(z_copied, 2 if nb < 2 else 3)
                cols = slice(nb * 512, (nb + 1) * 512)
                for m_ in range(4):
                    n = nb * 4 + m_
                    if n >= 2:
                        pe.wait_ge(h1_done, n - 1)
                    nc.tensor.matmul(ps[n % 2][:, 0, :], wt1a[:, m_ * 128:(m_ + 1) * 128], z12[:, cols], start=True, stop=False)
                    nc.tensor.matmul(ps[n % 2][:, 0, :], wt1b[:, m_ * 128:(m_ + 1) * 128], z0d[:, cols], start=False, stop=True)\
                        .then_inc(mm1_ready, 1)

            def layer2(nb):
                pe.wait_ge(h1_done, 4 * nb + 4)
                if nb == 0:
                    pe.wait_ge(z_copied, 3)
                else:
                    pe.wait_ge(h2_done, 2 * nb)
                for m_ in range(2):
                    for k in range(4):
                        m = nc.tensor.matmul(misc[m_][:, :], wt2[:, k, m_ * 128:(m_ + 1) * 128],
                                             h1[nb % 2][:, k * 512:(k + 1) * 512], start=k == 0, stop=k == 3)
                    m.then_inc(mm2_ready, 1)

            layer1(0)
            for nb in range(4):
                if nb + 1 < 4:
                    layer1(nb + 1)
                layer2(nb)
            pe.wait_ge(h2_done, 8)
            for k in range(2):
                for nb in range(4):
                    m = nc.tensor.matmul(acc1[32 * nb:32 * nb + 32, :], wt3[:, k:k + 1].broadcast_to([128, 32]),
                                         h2[nb][:, k * 512:(k + 1) * 512], start=k == 0, stop=k == 1)
            m.then_inc(mm3_ready, 1)


def selections(np):
    row_f = np.arange(KX) % F
    two = row_f[:, None, None] == (2 * np.arange(FC)[:, None] + np.arange(128)[None, :] // H)[None]
    m = np.arange(SHC * F)
    fields = [m % F] + [(m % F + SHC * c + m // F) % F for c in range(3)]
    one = np.stack([row_f[:, None] == f[None, :] for f in fields], axis=1)
    order = list(range(0, F, 2)) + list(range(1, F, 2))
    picks = np.zeros((128, sum(PICKS)), np.float32)
    picks[0:KX, 0:-128] = np.concatenate(
        [two.reshape(KX, -1), one.reshape(KX, -1), row_f[:, None] == np.array(order)[None, :]], axis=1)
    picks[:, -128:] = np.eye(128)
    own_row = np.zeros((128, CB), np.float32)
    own_row[:] = np.arange(128)[:, None] // D == np.arange(CB)[None, :]
    return {"picks": picks, "fold": np.concatenate([np.eye(H, dtype=np.float32)] * (128 // H)), "own_row": own_row}


def unordered_pairs():
    upper, lower = [], []
    for k in range(SH):
        for f in range(F if k < SH - 1 else F // 2):
            g = (f + k) % F
            upper.append(f * F + g)
            if k:
                lower.append(g * F + f)
    return upper, lower


def kernel(**inputs):
    import numpy as np
    import concourse.bacc as bacc
    from concourse.bass_utils import run_bass_kernel_spmd

    upper, lower = unordered_pairs()
    w0 = np.asarray(inputs["L0_rec_W0"])
    arrays = {
        "dense_t": np.ascontiguousarray(np.asarray(inputs["dense_ctx"]).T), "ids": inputs["ids"],
        "w0_upper": np.ascontiguousarray(w0[upper]), "w0_lower": np.ascontiguousarray(w0[lower]),
        "w1": inputs["L0_rec_W1"], "w2": inputs["L0_rec_W2"], "wt1": inputs["W_top1"], "wt2": inputs["W_top2"],
        "wt3": inputs["W_top3"].reshape(-1, 128).T, "bt1": inputs["b_top1"].reshape(-1, 128).T,
        "bt2": inputs["b_top2"].reshape(-1, 128).T,
    } | {f"table{f}": inputs[f"tbl_{f}"] for f in range(F)}
    arrays = {n: np.ascontiguousarray(a) for n, a in arrays.items()} | selections(np)
    nc = bacc.Bacc("TRN2", target_bir_lowering=False, num_devices=1)
    aps = {n: nc.dram_tensor(f"in_{n}", a.shape, mybir.dt.from_np(a.dtype), kind="ExternalInput").ap()
           for n, a in arrays.items()}
    aps["tables"] = [aps.pop(f"table{f}") for f in range(F)]
    aps["out"] = nc.dram_tensor("out", (B, 1), F32, kind="ExternalOutput").ap()
    tower(nc, aps)
    r = run_bass_kernel_spmd(nc, [{f"in_{n}": a for n, a in arrays.items()}], core_ids=[0])
    return r.results[0]["out"]
```

```python
from contextlib import ExitStack

import concourse.bass as bass
from concourse import mybir

F32 = mybir.dt.float32
BF16 = mybir.dt.bfloat16
I32 = mybir.dt.int32
U32 = mybir.dt.uint32
ALU = mybir.AluOpType
ACT = mybir.ActivationFunctionType
AX = mybir.AxisListType

B, F, D, H, DENSE = 2048, 24, 16, 64, 16
T1, T2 = 512, 256
TB = 128
TILES = B // TB
PAIRS = 2 * TILES
PB = TB // 2
COLS = PB * D
BLK = COLS // 2
BB = BLK // D
CH = COLS // 128
CB = 128 // D
PARTS = 3
KX = PARTS * F
SH = F // 2 + 1
SHC = 5
L0_ROWS = [SHC * F, SHC * F, (SH - 2 * SHC) * F]
FC = F // 2
GF = FC + 1
WIDE = 7
WIDE_LOADS = [(5, 7), (7, 9), (9, 11), (11, 12)]
GP = 4


def spread_schedule():
    one = [("one", c) for c in range(3)]
    two = [("two", c) for c in range(FC)]
    through_psum, by_dma = one + two[:FC - WIDE], two[FC - WIDE:]
    full = [step for both in zip(through_psum, by_dma + [None]) for step in both if step]
    return full, one, [step for step in full if step[0] == "two"]


FULL, FIRST, LAST = spread_schedule()
PER_SLOT = len(FULL)
SPREADS = PER_SLOT - WIDE
SUM_AT = 7
LAG = 1
NZ = 5
PICKS = [FC * 128, 3 * SHC * F, F, 128]


class Slot:

    def __init__(self, q, r, number=None):
        self.q, self.r = q, r
        n = number
        self.one = n is None or n < PAIRS
        self.two = n is None or 1 <= n <= PAIRS
        self.gram = n is None or 2 <= n
        self.steps = FULL if self.one and self.two else FIRST if self.one else LAST if self.two else []
        self.split = n != 0 and (r % 2 == 0 or n == 1) and (n is None or n <= PAIRS - 4)
        self.turn = r % 2 == 1 and (n is None or n <= PAIRS - 3)
        self.group_ends = self.gram and (r - 2) % GP == GP - 1
        self.number = n
        self.done = 0 if n == 0 else q * PER_SLOT - (PER_SLOT - 3)
        self.spreads_done = 0 if n == 0 else q * SPREADS - (SPREADS - 3)
        self.spread_at = [p for p, step in enumerate(self.steps) if step[0] == "one" or step[1] < FC - WIDE]

    def nth(self, pos):
        return self.done + (pos + 1)

    def of(self, kind):
        return [p for p, step in enumerate(self.steps) if step[0] == kind]

    def nth_spread(self, pos):
        return self.spreads_done + (self.spread_at.index(pos) + 1)

    def place(self, pos):
        return (self.spread_at.index(pos) + (self.number != 0)) % 2

    def buffer(self, pos):
        return (pos + (3 if self.number != 0 else 0)) % NZ


assert PER_SLOT % NZ == 0 and SPREADS % 2 == 0


def tower(nc, x):
    with ExitStack() as ctx:
        def sb(name, shape, dt=F32):
            return ctx.enter_context(nc.sbuf_tensor(name, shape, dt))

        def sem(name):
            return ctx.enter_context(nc.semaphore(name))

        w0a = sb("w0a", [SHC * F, 3, H])
        w0b = sb("w0b", [SHC * F, 3, H])
        w1 = sb("w1", [128, FC, H])
        w2 = sb("w2", [128, FC, H])
        wt1a = sb("wt1a", [2 * H, T1])
        wt1b = sb("wt1b", [H + DENSE, T1])
        wt2 = sb("wt2", [128, T1 // 128, T2])
        wt3 = sb("wt3", [128, T2 // 128])
        bt1 = sb("bt1", [128, T1 // 128])
        bt2 = sb("bt2", [128, T2 // 128])
        picks = sb("picks", [128, sum(PICKS)], BF16)
        at = [sum(PICKS[:n]) for n in range(len(PICKS) + 1)]
        spread_two = picks[0:KX, at[0]:at[1]].rearrange("k (c m) -> k c m", c=FC)
        spread_one = picks[0:KX, at[1]:at[2]].rearrange("k (c m) -> k c m", c=3)
        collect = picks[0:KX, at[2]:at[3]]
        ident = picks[:, at[3]:at[4]]
        ident_f32 = sb("ident_f32", [128, 128])
        own_row = sb("own_row", [128, CB])
        idx = sb("idx", [128, 2, F], I32)
        emb = sb("emb", [TB, 2, F, D])
        rest = sb("rest", [TB, F, D])
        parts = sb("parts", [TB, D, PARTS, F], BF16)
        x0s = sb("x0s", [KX, 2, TB * D], BF16)
        rep = sb("rep", [SHC * F, 2, COLS])
        prod = sb("prod", [128, NZ, 2, BLK])
        x1 = sb("x1", [128, 2, COLS])
        x2 = sb("x2", [128, BLK])
        x2t = sb("x2t", [128, CH // 2, 2, H])
        x0t = sb("x0t", [128, 2, CH, F])
        diag = sb("diag", [128, 2, CH, CB, 1 + F])
        sum1 = sb("sum1", [128, PAIRS * BB])
        gram = sb("gram", [128, GF, GP * PB])
        wide = sb("wide", [128, 2, WIDE, COLS])
        z12 = sb("z12", [2 * H, B])
        z0d = sb("z0d", [H + DENSE, B])
        h1 = [x1[:].rearrange("p a c -> p (a c)"),
              diag[:].rearrange("p a c b f -> p (a c b f)")[:, 0:4 * 512]]
        h2 = [sb(f"h2{n}", [128, 2 * 512])[:, :] for n in range(2)] + [prod[:, n].rearrange("p b c -> p (b c)") for n in range(2)]
        y = sb("y", [128, 512])

        ps = [ctx.enter_context(nc.psum_tensor(f"spread{i}", [128, 2, BLK], F32)) for i in range(2)]
        acc1 = ctx.enter_context(nc.psum_tensor("acc1", [128, BLK], F32))
        acc2 = ctx.enter_context(nc.psum_tensor("acc2", [128, BLK], F32))
        misc = [ctx.enter_context(nc.psum_tensor(f"misc{i}", [128, BLK], F32)) for i in range(2)]

        weights_in = sem("weights_in")
        ids_in = [sem(f"ids_in{i}") for i in range(2)]
        gathered = [sem(f"gathered{i}") for i in range(2)]
        stored = sem("stored")
        w0_zeroed, w0_summed = sem("w0_zeroed"), sem("w0_summed")
        diag_ones, picks_done = sem("diag_ones"), sem("picks_done")
        hi_done, rest_done, mid_done, lo_done = sem("hi_done"), sem("rest_done"), sem("mid_done"), sem("lo_done")
        turned, turn_copied = sem("turned"), sem("turn_copied")
        rep_in = [sem(f"rep_in{i}") for i in range(2)]
        spread = sem("spread")
        multiplied = sem("multiplied")
        contracted = sem("contracted")
        acc1_summed, x1_copied, x2_copied = sem("acc1_summed"), sem("x1_copied"), sem("x2_copied")
        x0t_ready, x0t_copied = sem("x0t_ready"), sem("x0t_copied")
        diag_done = sem("diag_done")
        x2t_ready, x2t_copied = sem("x2t_ready"), sem("x2t_copied")
        gram_ready, gram_copied = sem("gram_ready"), sem("gram_copied")
        out2_ready, z12_copied, z0_copied = sem("out2_ready"), sem("z12_copied"), sem("z0_copied")
        x0_stored = sem("x0_stored")
        wide_in = [sem(f"wide_in{i}") for i in range(2)]
        mm1_ready, h1_done = sem("mm1_ready"), sem("h1_done")
        mm2_ready, h2_done = sem("mm2_ready"), sem("h2_done")
        mm3_ready, y_done = sem("mm3_ready"), sem("y_done")

        picks_f32 = prod[:].rearrange("p a b c -> p (a b c)")[:, 0:sum(PICKS)]
        loads = [
            (picks_f32, x["picks"]), (ident_f32[:, :], x["picks"][:, -128:]), (own_row[:, :], x["own_row"]),
        ]
        loads += [(w0a[0:SHC * F, c, :], x["w0_upper"][c * SHC * F:(c + 1) * SHC * F, :]) for c in range(2)]
        loads += [(w0a[0:L0_ROWS[2], 2, :], x["w0_upper"][2 * SHC * F:, :])]
        loads += [(w0b[F:SHC * F, 0, :], x["w0_lower"][0:(SHC - 1) * F, :]),
                  (w0b[0:SHC * F, 1, :], x["w0_lower"][(SHC - 1) * F:(2 * SHC - 1) * F, :]),
                  (w0b[0:L0_ROWS[2] - F, 2, :], x["w0_lower"][(2 * SHC - 1) * F:, :])]
        loads += [(w1[:, :, :], x["w1"].rearrange("(c p) o -> p c o", p=128))]
        loads += [(w2[:, :, :], x["w2"].rearrange("(c p) o -> p c o", p=128))]
        loads += [(wt1a[:, :], x["wt1"][H:3 * H, :]), (wt1b[0:H, :], x["wt1"][0:H, :]),
                  (wt1b[H:H + DENSE, :], x["wt1"][3 * H:3 * H + DENSE, :]),
                  (z0d[H:H + DENSE, :], x["dense_t"]), (wt2[:, :, :], x["wt2"].rearrange("(c p) n -> p c n", p=128)),
                  (wt3[:, :], x["wt3"]), (bt1[:, :], x["bt1"]), (bt2[:, :], x["bt2"])]
        ALL_LOADED = 16 * len(loads)

        def gathers_of(tile):
            return 16 * F * (tile // 2 + 1)

        def wide_loads(p):
            return 16 * 2 * len(WIDE_LOADS) * (p // 2 + 1)

        def rep_loads(p):
            return 16 * SHC * (p // 2 + 1)

        block = ctx.enter_context(nc.Block())

        @block.sync
        def _(sp):
            def fetch_ids(s, tile, before):
                sp.wait_ge(gathered[s], before)
                sp.dma_start(idx[:, s, :], x["ids"][bass.ds(tile * TB, TB), :]).then_inc(ids_in[s], 16)

            def store_x0(s, tile, gathered_value):
                sp.wait_ge(gathered[s], gathered_value)
                sp.dma_start(x["x0_rows"].rearrange("f (b d) -> b f d", d=D)[bass.ds(tile * TB, TB)], emb[:, s])\
                  .then_inc(x0_stored, 16)
                sp.wait_ge(x0_stored, tile * 16 + 16)

            def load_rep(p, parity):
                for k in range(SHC):
                    sp.dma_start(rep[k * F:(k + 1) * F, parity, :], x["x0_rows"][:, bass.ds(p * COLS, COLS)])\
                      .then_inc(rep_in[parity], 16)

            def load_wide(p, parity):
                rows = x["x0_rows"].rearrange("(c h) n -> h c n", h=2)
                for first, end in WIDE_LOADS:
                    for half in range(2):
                        src = rows[half:half + 1, first:end, bass.ds(p * COLS, COLS)].broadcast_to([H, end - first, COLS])
                        sp.dma_start(wide[H * half:H * half + H, parity, first - (FC - WIDE):end - (FC - WIDE), :], src)\
                          .then_inc(wide_in[parity], 16)

            for t in range(2):
                sp.dma_start(idx[:, t, :], x["ids"][t * TB:(t + 1) * TB, :]).then_inc(ids_in[t], 16)
            for dst, src in loads:
                sp.dma_start(dst, src).then_inc(weights_in, 16)
            store_x0(0, 0, gathers_of(0))
            load_rep(0, 0)
            fetch_ids(0, 2, gathers_of(0))
            load_rep(1, 1)
            load_wide(0, 0)
            load_wide(1, 1)
            store_x0(1, 1, gathers_of(1))
            sp.wait_ge(multiplied, 3)
            load_rep(2, 0)
            fetch_ids(1, 3, gathers_of(1))

            def slot_loads(p, r, tile, gathered_value, ids, last):
                sp.wait_ge(multiplied, p * PER_SLOT - (PER_SLOT - 3))
                load_wide(p, r % 2)
                if tile is not None:
                    s = (r // 2 + 1) % 2
                    store_x0(s, tile, gathered_value)
                if not last:
                    load_rep(p + 1, (r + 1) % 2)
                if ids:
                    fetch_ids(s, tile + 2, gathered_value)

            with sp.Fori(0, (PAIRS - 8) // 4) as i:
                for j in range(4):
                    odd = j % 2 == 1
                    slot_loads(i * 4 + (2 + j), (2 + j) % 4, i * 2 + (3 + j) // 2 if odd else None,
                               i * (16 * F) + 16 * F * ((3 + j) // 4 + 1), odd, False)
            for p in range(PAIRS - 6, PAIRS):
                tile = (p + 1) // 2 if p % 2 and p < PAIRS - 1 else None
                slot_loads(p, p % 4, tile, gathers_of(tile) if tile else None, False, p == PAIRS - 1)
            sp.wait_ge(y_done, 1)
            sp.dma_start(x["out"].rearrange("(n b) a -> n (b a)", n=4), y[0:128:32, :]).then_inc(stored, 16)
            sp.wait_ge(stored, 16)

        @block.gpsimd
        def _(pool):
            def gather(s, first, last):
                for f in range(first, last):
                    nc.gpsimd.indirect_dma_start(
                        out=emb[:, s, f, :], out_offset=None, in_=x["tables"][f],
                        in_offset=bass.IndirectOffsetOnAxis(ap=idx[:, s, f:f + 1].bitcast(U32), axis=0),
                    ).then_inc(gathered[s], 16)

            def diagonals(slot):
                q, s = slot.q, (slot.r - 1) % 2
                pool.wait_ge(x0t_copied, q)
                if slot.gram:
                    pool.wait_ge(gram_ready, q * 2 - 3)
                nc.gpsimd.tensor_tensor(
                    diag[:, s, :, :, 1:1 + F], x0t[:, s, :, :].unsqueeze(2).broadcast_to([128, CH, CB, F]),
                    own_row[:, :].unsqueeze(1).unsqueeze(3).broadcast_to([128, CH, CB, F]), ALU.mult,
                ).then_inc(diag_done, 1)

            for s in range(2):
                pool.wait_ge(ids_in[s], 16)
                gather(s, 0, F)
            pool.wait_ge(weights_in, ALL_LOADED)
            for s in range(2):
                nc.gpsimd.tensor_copy(diag[:, s, :, :, 0],
                                      own_row[:, :].unsqueeze(1).broadcast_to([128, CH, CB])).then_inc(diag_ones, 1)

            def slot_work(slot, fetch):
                s, half = slot.r // 2, slot.r % 2
                if fetch and half == 0:
                    if slot.number is None:
                        ids_value, rest_value = fetch
                    else:
                        t = slot.q // 2
                        ids_value, rest_value = 16 * ((t + 2) // 2 + 1), t + 1
                    pool.wait_ge(ids_in[s], ids_value)
                    pool.wait_ge(rest_done, rest_value)
                    pool.wait_ge(x0_stored, rest_value * 16)
                if slot.two:
                    diagonals(slot)
                if fetch:
                    gather(s, *((14, F) if half else (0, 14)))

            slot_work(Slot(0, 0, 0), True)
            slot_work(Slot(1, 1, 1), True)
            with pool.Fori(0, (PAIRS - 8) // 4) as i:
                for j in range(4):
                    t0 = 1 + j // 2
                    slot_work(Slot(i * 4 + (2 + j), (2 + j) % 4),
                              (i * 16 + 16 * ((t0 + 2) // 2 + 1), i * 2 + (t0 + 1)))
            for n in range(PAIRS - 6, PAIRS + 1):
                slot_work(Slot(n, n % 4, n), n < PAIRS - 4)

        @block.scalar
        def _(act):
            copy = ACT.Copy

            def split_hi(s, gathered_value, turned_value):
                act.wait_ge(gathered[s], gathered_value)
                if turned_value is not None:
                    act.wait_ge(turned, turned_value)
                nc.scalar.activation(parts[:, :, 0, :].rearrange("p d f -> p f d"), emb[:, s, :, :], copy)\
                    .then_inc(hi_done, 1)

            def split_mid(rest_value):
                act.wait_ge(rest_done, rest_value)
                nc.scalar.activation(parts[:, :, 1, :].rearrange("p d f -> p f d"), rest[:, :, :], copy)\
                    .then_inc(mid_done, 1)

            def copy_turned(s, g, value):
                act.wait_ge(turned, value)
                nc.scalar.activation(
                    x0s[:, s, :].rearrange("k (b d) -> k d b", d=D)[:, g * 8:g * 8 + 8, :],
                    misc[g][0:KX, :].bitcast(BF16).rearrange("k (d b) -> k d b", b=TB), copy,
                ).then_inc(turn_copied, 1)

            def copy_x1(slot):
                act.wait_ge(acc1_summed, slot.q + 1)
                for blk in range(2):
                    for half in range(2):
                        c = nc.scalar.activation(x1[H * half:H * half + H, slot.r % 2, blk * BLK:(blk + 1) * BLK],
                                                 acc1[H * blk:H * blk + H, :], copy)
                c.then_inc(x1_copied, 1)

            def copy_x2(slot):
                act.wait_ge(contracted, slot.nth(slot.of("two")[-1]))
                nc.scalar.activation(x2[:, :], acc2[:, :], copy).then_inc(x2_copied, 1)

            def copy_gram(slot, part):
                q = slot.q
                act.wait_ge(gram_ready, q * 2 + (part - 3))
                cols = CH // 2 * CB
                first = (slot.r - 2) % GP * PB + part * cols
                nc.scalar.activation(
                    gram[:, :, first:first + cols].rearrange("p f (c b) -> p c b f", b=CB),
                    misc[part][:, 0:cols * GF].rearrange("p (c b f) -> p c b f", b=CB, f=GF), copy,
                ).then_inc(gram_copied, 1)

            def copy_sum1():
                z0 = z0d[0:H, :].rearrange("p (q k b) -> p k q b", k=2, b=BB)
                for k in range(2):
                    last = nc.scalar.activation(z0[:, k], sum1[H * k:H * k + H, :].rearrange("p (q b) -> p q b", b=BB), copy)
                last.then_inc(z0_copied, 1)

            def hidden1(nb):
                for m in range(T1 // 128):
                    n = nb * (T1 // 128) + m
                    act.wait_ge(mm1_ready, n + 1)
                    if m == 0 and nb >= 2:
                        act.wait_ge(mm2_ready, 2 * (nb - 1))
                    nc.scalar.activation(h1[nb % 2][:, m * 512:(m + 1) * 512], ps[n % 2][:, 0, :], ACT.Relu,
                                         bias=bt1[:, m:m + 1]).then_inc(h1_done, 1)

            def copy_out2(g):
                act.wait_ge(out2_ready, g + 1)
                for k in range(2):
                    half = GP * PB // 2
                    nc.scalar.activation(z12[H:2 * H, bass.ds(g * (GP * PB) + k * half, half)],
                                         misc[0][H * k:H * k + H, 0:half], copy)
                nc.scalar.activation(z12[0:H, bass.ds(g * (GP * PB), GP * PB)], gram[0:H, 0, :], copy)\
                    .then_inc(z12_copied, 1)

            def slot_work(slot, gathered_value, group):
                q, r = slot.q, slot.r
                tile_s = (1 if slot.number == 1 else r // 2 + 1) % 2
                if slot.two:
                    act.wait_ge(x0t_ready, q)
                    if slot.number != 1:
                        act.wait_ge(diag_done, q - 1)
                    nc.scalar.activation(x0t[:, (r - 1) % 2, :, :], misc[0][:, 0:CH * F].rearrange("p (c f) -> p c f", f=F),
                                         copy).then_inc(x0t_copied, 1)
                if slot.gram:
                    act.wait_ge(x2t_ready, q - 1)
                    nc.scalar.activation(x2t[:, :, :, :].rearrange("p c k o -> p (c k o)"), misc[1][:, :], copy)\
                        .then_inc(x2t_copied, 1)
                    if not slot.two:
                        hidden1(0)
                if slot.split:
                    T = 1 if slot.number == 1 else None
                    split_hi(tile_s, gathered_value, 2 if T else q + 2)
                if slot.gram:
                    copy_gram(slot, 0)
                    copy_gram(slot, 1)
                if slot.split:
                    split_mid(2 if slot.number == 1 else T_of(slot))
                if slot.turn:
                    copy_turned(((r + 1) // 2) % 2, 0, q + 2)
                    copy_turned(((r + 1) // 2) % 2, 1, q + 3)
                if slot.one:
                    copy_x1(slot)
                if slot.gram and not slot.two:
                    hidden1(1)
                if slot.group_ends:
                    copy_out2(group)
                if slot.two:
                    copy_x2(slot)

            def T_of(slot):
                return slot.half + 2 if slot.half is not None else slot.q // 2 + 2

            act.wait_ge(weights_in, ALL_LOADED)
            nc.scalar.activation(picks[:, :], picks_f32, copy).then_inc(picks_done, 1)
            split_hi(0, gathers_of(0), None)
            split_mid(1)
            copy_turned(0, 0, 1)
            copy_turned(0, 1, 2)
            for n in (0, 1):
                slot = Slot(n, n, n)
                slot.half = None
                slot_work(slot, gathers_of(1), None)
            with act.Fori(0, (PAIRS - 4) // 4) as i:
                for j in range(4):
                    slot = Slot(i * 4 + (2 + j), (2 + j) % 4)
                    slot.half = i * 2 + (1 + j // 2)
                    slot_work(slot, i * (16 * F) + 16 * F * ((2 + j // 2) // 2 + 1), i)
            for n in range(PAIRS - 2, PAIRS + 2):
                slot = Slot(n, n % 4, n)
                slot.half = None
                slot_work(slot, None, PAIRS // GP - 1)
                if n == PAIRS:
                    copy_sum1()

            hidden1(2)
            hidden1(3)

        @block.vector
        def _(dve):
            def split_rest(s, hi_value):
                dve.wait_ge(hi_done, hi_value)
                nc.vector.tensor_tensor(rest[:, :, :], emb[:, s, :, :], parts[:, :, 0, :].rearrange("p d f -> p f d"),
                                        ALU.subtract).then_inc(rest_done, 1)

            def split_lo(mid_value):
                dve.wait_ge(mid_done, mid_value)
                nc.vector.tensor_tensor(parts[:, :, 2, :].rearrange("p d f -> p f d"), rest[:, :, :],
                                        parts[:, :, 1, :].rearrange("p d f -> p f d"), ALU.subtract)\
                    .then_inc(lo_done, 1)

            def product(slot, pos, step):
                nth = slot.nth(pos)
                if slot.number is None or nth - NZ > 0:
                    dve.wait_ge(contracted, nth - NZ)
                through_psum = pos in slot.spread_at
                if through_psum:
                    dve.wait_ge(spread, slot.nth_spread(pos))
                    operand = ps[slot.place(pos)][:, :, :].rearrange("p a c -> p (a c)")
                dst = prod[:, slot.buffer(pos)]
                if step[0] == "one":
                    if step[1] == 0:
                        dve.wait_ge(rep_in[slot.r % 2], slot.rep_value)
                    rows = L0_ROWS[step[1]]
                    nc.vector.tensor_tensor(dst[0:rows].rearrange("p a c -> p (a c)"), operand[0:rows],
                                            rep[0:rows, slot.r % 2, :], ALU.mult).then_inc(multiplied, 1)
                else:
                    if pos == slot.of("two")[0]:
                        dve.wait_ge(x1_copied, slot.q)
                    if not through_psum:
                        if pos == min(set(slot.of("two")) - set(slot.spread_at)):
                            dve.wait_ge(wide_in[(slot.r - 1) % 2], slot.wide_value)
                        operand = wide[:, (slot.r - 1) % 2, step[1] - (FC - WIDE), :]
                    nc.vector.tensor_tensor(dst.rearrange("p a c -> p (a c)"), operand, x1[:, (slot.r - 1) % 2, :], ALU.mult).then_inc(multiplied, 1)

            def sum_x1(slot):
                dve.wait_ge(contracted, slot.nth(slot.of("one")[-1]))
                nc.vector.tensor_reduce(sum1[:, bass.ds(slot.q * BB, BB)], acc1[:, :].rearrange("p (b d) -> p b d", d=D),
                                        AX.X, ALU.add).then_inc(acc1_summed, 1)

            def slot_work(slot):
                T = None
                for pos, step in enumerate(slot.steps):
                    product(slot, pos, step)
                    if slot.split and pos == (2 if slot.number == 1 else 5):
                        split_rest(slot.split_s, slot.split_value)
                    if slot.split and pos == (6 if slot.number == 1 else 10):
                        split_lo(slot.split_value)
                    if slot.one and pos == (SUM_AT if slot.steps is FULL else 2):
                        sum_x1(slot)

            nc.vector.memset(w0b[0:F, 0, :], 0.0).then_inc(w0_zeroed, 1)
            dve.wait_ge(weights_in, ALL_LOADED)
            dve.wait_ge(w0_zeroed, 1)
            nc.vector.tensor_tensor(w0a[:, 0:2, :], w0a[:, 0:2, :], w0b[:, 0:2, :], ALU.add).then_inc(w0_summed, 1)
            last = L0_ROWS[2] - F
            nc.vector.tensor_tensor(w0a[0:last, 2, :], w0a[0:last, 2, :], w0b[0:last, 2, :], ALU.add)\
                .then_inc(w0_summed, 1)
            split_rest(0, 1)
            split_lo(1)
            for n in (0, 1):
                slot = Slot(n, n, n)
                slot.split_s, slot.split_value, slot.wide_value = 1, 2, wide_loads(0)
                slot.rep_value = rep_loads(n)
                slot_work(slot)
            with dve.Fori(0, (PAIRS - 4) // 4) as i:
                for j in range(4):
                    slot = Slot(i * 4 + (2 + j), (2 + j) % 4)
                    slot.split_s = (j // 2) % 2
                    slot.split_value = i * 2 + (3 + j // 2)
                    slot.wide_value = i * (2 * wide_loads(0)) + wide_loads(1 + j)
                    slot.rep_value = i * (2 * rep_loads(0)) + rep_loads(2 + j)
                    slot_work(slot)
            for n in range(PAIRS - 2, PAIRS + 2):
                slot = Slot(n, n % 4, n)
                slot.wide_value, slot.rep_value = wide_loads(n - 1), rep_loads(n)
                slot_work(slot)

            for nb in range(4):
                for m in range(2):
                    dve.wait_ge(mm2_ready, 2 * nb + m + 1)
                    nc.vector.tensor_scalar(h2[nb][:, m * 512:(m + 1) * 512], ps[m][:, 1, :], bt2[:, m:m + 1], 0.0,
                                            ALU.add, ALU.max).then_inc(h2_done, 1)
            dve.wait_ge(mm3_ready, 1)
            nc.vector.tensor_copy(y[:, :], acc1[:, :]).then_inc(y_done, 1)

        @block.tensor
        def _(pe):
            def turn(s_group, value):
                g = s_group
                if g == 0:
                    pe.wait_ge(lo_done, value)
                dst = misc[g][0:KX, :].bitcast(BF16)
                for k in range(8):
                    m = nc.tensor.transpose(dst[:, k * TB:(k + 1) * TB],
                                            parts[:, g * 8 + k, :, :].rearrange("b p f -> b (p f)"), ident[:, :])
                m.then_inc(turned, 1)

            def spread_into(slot, pos):
                step = slot.steps[pos]
                dst = ps[slot.place(pos)]
                if step[0] == "two":
                    r = (slot.r - 1) % 4
                    base = (r % 2) * COLS
                    for blk in range(2):
                        m = nc.tensor.matmul(dst[:, blk, :], spread_two[:, step[1], :],
                                             x0s[:, r // 2, base + blk * BLK:base + (blk + 1) * BLK], start=True, stop=True)
                    m.then_inc(spread, 1)
                    return
                c, rows = step[1], L0_ROWS[step[1]]
                if c == 0 and slot.r % 2 == 0:
                    pe.wait_ge(turn_copied, slot.q + 2)
                base = (slot.r % 2) * COLS
                for blk in range(2):
                    m = nc.tensor.matmul(dst[0:rows, blk, :], spread_one[:, c, 0:rows],
                                         x0s[:, slot.r // 2, base + blk * BLK:base + (blk + 1) * BLK], start=True, stop=True)
                m.then_inc(spread, 1)

            def contract(slot, pos):
                step, z = slot.steps[pos], prod[:, slot.buffer(pos)]
                if step[0] == "one":
                    c, rows = step[1], L0_ROWS[step[1]]
                    if c == 0 and (slot.number is None or slot.number > 0):
                        pe.wait_ge(x1_copied, slot.q)
                    for blk in range(2):
                        m = nc.tensor.matmul(acc1[H * blk:H * blk + H, :], w0a[0:rows, c, :], z[0:rows, blk, :],
                                             start=c == 0, stop=c == 2)
                    m.then_inc(contracted, 1)
                    return
                steps = slot.of("two")
                if pos == steps[0] and slot.number != 1:
                    pe.wait_ge(x2_copied, slot.q - 1)
                for blk in range(2):
                    m = nc.tensor.matmul(acc2[H * blk:H * blk + H, :], w1[:, step[1], :], z[:, blk, :],
                                         start=pos == steps[0], stop=pos == steps[-1])
                m.then_inc(contracted, 1)

            def gram_before(slot):
                return slot.number >= PAIRS if slot.number is not None and slot.r % 2 == 0 else slot.r % 2 == 1 and slot.number != 1

            def collect_x0t(slot):
                r = (slot.r - 1) % 4
                if gram_before(slot):
                    pe.wait_ge(gram_copied, slot.q * 2 - 5)
                for c in range(CH):
                    base = (r % 2) * COLS + c * 128
                    m = nc.tensor.matmul(misc[0][:, c * F:(c + 1) * F], x0s[:, r // 2, base:base + 128], collect[:, :],
                                         start=True, stop=True)
                m.then_inc(x0t_ready, 1)

            def turn_x2(slot):
                q = slot.q
                pe.wait_ge(x2_copied, q - 1)
                if gram_before(slot):
                    pe.wait_ge(gram_copied, q * 2 - 4)
                for c in range(CH // 2):
                    m = nc.tensor.transpose(misc[1][:, c * 128:(c + 1) * 128], x2[:, c * 128:(c + 1) * 128], ident_f32[:, :])
                m.then_inc(x2t_ready, 1)

            def gram_of(slot, part):
                q, s = slot.q, slot.r % 2
                if part == 0:
                    pe.wait_ge(x2t_copied, q - 1)
                    pe.wait_ge(diag_done, q - 1)
                    if slot.two:
                        pe.wait_ge(x0t_copied, q)
                    else:
                        pe.wait_ge(gram_copied, q * 2 - 5)
                width = CB * GF
                for c in range(CH // 2):
                    for odd in range(2):
                        ch = part * (CH // 2) + c
                        m = nc.tensor.matmul(misc[part][H * odd:H * odd + H, c * width:(c + 1) * width], x2t[:, c, part, :],
                                             diag[:, s, ch, :, FC * odd:FC * odd + GF], start=True, stop=True)
                m.then_inc(gram_ready, 1)

            def sum_group(slot):
                pe.wait_ge(gram_copied, slot.q * 2 - 2)
                if slot.turn:
                    pe.wait_ge(turn_copied, slot.q + 2)
                half = GP * PB // 2
                for c in range(FC):
                    for k in range(2):
                        m = nc.tensor.matmul(misc[0][H * k:H * k + H, 0:half], w2[:, c, :],
                                             gram[:, 1 + c, k * half:(k + 1) * half], start=c == 0, stop=c == FC - 1)
                m.then_inc(out2_ready, 1)

            def layer1(nb):
                if nb == 0:
                    pe.wait_ge(z0_copied, 1)
                if nb == 3:
                    pe.wait_ge(z12_copied, PAIRS // GP)
                cols = slice(nb * 512, (nb + 1) * 512)
                for m_ in range(4):
                    n = nb * 4 + m_
                    if n >= 2:
                        pe.wait_ge(h1_done, n - 1)
                    nc.tensor.matmul(ps[n % 2][:, 0, :], wt1a[:, m_ * 128:(m_ + 1) * 128], z12[:, cols], start=True, stop=False)
                    nc.tensor.matmul(ps[n % 2][:, 0, :], wt1b[:, m_ * 128:(m_ + 1) * 128], z0d[:, cols], start=False, stop=True)\
                        .then_inc(mm1_ready, 1)

            def slot_work(before, slot, after, lo_value, group=None):
                q = slot.q
                count = len(slot.steps)
                for pos in range(max(count, 1)):
                    if slot.steps:
                        pe.wait_ge(multiplied, slot.nth(pos))
                        if pos in slot.spread_at:
                            ahead = slot.spread_at.index(pos) + 2
                            if ahead < len(slot.spread_at):
                                spread_into(slot, slot.spread_at[ahead])
                            elif after.steps:
                                spread_into(after, after.spread_at[ahead - len(slot.spread_at)])
                    if pos < LAG and before is not None:
                        for late in ([pos] if count else range(LAG)):
                            contract(before, len(before.steps) - LAG + late)
                    if LAG <= pos < count:
                        contract(slot, pos - LAG)
                    if slot.number == 0 and pos == count - 1:
                        for late in range(LAG):
                            contract(slot, count - LAG + late)
                    if pos == 0 and slot.two:
                        collect_x0t(slot)
                    if slot.gram and pos == (1 if count else 0):
                        turn_x2(slot)
                        if not count:
                            layer1(0)
                    if slot.gram and pos == (3 if count else 0):
                        gram_of(slot, 0)
                    if slot.gram and pos == (4 if count else 0):
                        gram_of(slot, 1)
                        if not count:
                            layer1(1)
                    if slot.turn and pos == (8 if slot.number == 1 else 7):
                        if slot.gram:
                            pe.wait_ge(gram_copied, q * 2 - 3)
                        else:
                            pe.wait_ge(x0t_copied, q)
                        turn(0, lo_value)
                    if slot.turn and pos == (9 if slot.number == 1 else 8):
                        if slot.gram:
                            pe.wait_ge(gram_copied, q * 2 - 2)
                        turn(1, None)
                    if slot.group_ends and pos == (11 if count else 0):
                        sum_group(slot)
                    if slot.group_ends and count and pos == count - 1:
                        pe.wait_ge(z12_copied, group + 1)

            pe.wait_ge(weights_in, ALL_LOADED)
            pe.wait_ge(picks_done, 1)
            turn(0, 1)
            turn(1, None)
            pe.wait_ge(turn_copied, 2)
            first, second = Slot(0, 0, 0), Slot(1, 1, 1)
            spread_into(first, 0)
            spread_into(first, 1)
            pe.wait_ge(w0_summed, 2)
            slot_work(None, first, second, None)
            slot_work(None, second, Slot(2, 2, 2), 2)
            with pe.Fori(0, (PAIRS - 4) // 4) as i:
                for j in range(4):
                    slot_work(Slot(i * 4 + (1 + j), (1 + j) % 4), Slot(i * 4 + (2 + j), (2 + j) % 4), Slot(i * 4 + (3 + j), (3 + j) % 4),
                              i * 2 + ((3 + j) // 2 + 1), i)
            for n in range(PAIRS - 2, PAIRS + 2):
                slot_work(Slot(n - 1, (n - 1) % 4, n - 1), Slot(n, n % 4, n), Slot(n + 1, (n + 1) % 4, n + 1), None, PAIRS // GP - 1)

            def layer2(nb):
                pe.wait_ge(h1_done, 4 * nb + 4)
                if nb > 0:
                    pe.wait_ge(h2_done, 2 * nb)
                for m_ in range(2):
                    for k in range(4):
                        m = nc.tensor.matmul(ps[m_][:, 1, :], wt2[:, k, m_ * 128:(m_ + 1) * 128],
                                             h1[nb % 2][:, k * 512:(k + 1) * 512], start=k == 0, stop=k == 3)
                    m.then_inc(mm2_ready, 1)

            for nb in range(4):
                layer2(nb)
                if nb + 2 < 4:
                    layer1(nb + 2)
            pe.wait_ge(h2_done, 8)
            for k in range(2):
                for nb in range(4):
                    m = nc.tensor.matmul(acc1[32 * nb:32 * nb + 32, :], wt3[:, k:k + 1].broadcast_to([128, 32]),
                                         h2[nb][:, k * 512:(k + 1) * 512], start=k == 0, stop=k == 1)
            m.then_inc(mm3_ready, 1)


def selections(np):
    row_f = np.arange(KX) % F
    two = row_f[:, None, None] == (2 * np.arange(FC)[:, None] + np.arange(128)[None, :] // H)[None]
    m = np.arange(SHC * F)
    fields = [(m % F + SHC * c + m // F) % F for c in range(3)]
    one = np.stack([row_f[:, None] == f[None, :] for f in fields], axis=1)
    order = list(range(0, F, 2)) + list(range(1, F, 2))
    picks = np.zeros((128, sum(PICKS)), np.float32)
    picks[0:KX, 0:-128] = np.concatenate(
        [two.reshape(KX, -1), one.reshape(KX, -1), row_f[:, None] == np.array(order)[None, :]], axis=1)
    picks[:, -128:] = np.eye(128)
    own_row = np.zeros((128, CB), np.float32)
    own_row[:] = np.arange(128)[:, None] // D == np.arange(CB)[None, :]
    return {"picks": picks, "own_row": own_row}


def unordered_pairs(np):
    fields = np.arange(F)
    shifted = [(fields + k) % F for k in range(SH)]
    upper = np.concatenate([fields * F + g for g in shifted])
    lower = np.concatenate([g * F + fields for g in shifted[1:-1]])
    return upper, lower


def kernel(**inputs):
    import numpy as np
    import concourse.bacc as bacc
    from concourse.bass_utils import run_bass_kernel_spmd

    upper, lower = unordered_pairs(np)
    w0 = np.asarray(inputs["L0_rec_W0"])
    arrays = {
        "dense_t": np.ascontiguousarray(np.asarray(inputs["dense_ctx"]).T), "ids": inputs["ids"],
        "w0_upper": np.ascontiguousarray(w0[upper]), "w0_lower": np.ascontiguousarray(w0[lower]),
        "w1": inputs["L0_rec_W1"], "w2": inputs["L0_rec_W2"], "wt1": inputs["W_top1"], "wt2": inputs["W_top2"],
        "wt3": inputs["W_top3"].reshape(-1, 128).T, "bt1": inputs["b_top1"].reshape(-1, 128).T,
        "bt2": inputs["b_top2"].reshape(-1, 128).T,
    } | {f"table{f}": inputs[f"tbl_{f}"] for f in range(F)}
    arrays = {n: np.ascontiguousarray(a) for n, a in arrays.items()} | selections(np)
    nc = bacc.Bacc("TRN2", target_bir_lowering=False, num_devices=1)
    aps = {n: nc.dram_tensor(f"in_{n}", a.shape, mybir.dt.from_np(a.dtype), kind="ExternalInput").ap()
           for n, a in arrays.items()}
    aps["tables"] = [aps.pop(f"table{f}") for f in range(F)]
    aps["x0_rows"] = nc.dram_tensor("x0_rows", (F, B * D), F32, kind="Internal").ap()
    aps["out"] = nc.dram_tensor("out", (B, 1), F32, kind="ExternalOutput").ap()
    tower(nc, aps)
    r = run_bass_kernel_spmd(nc, [{f"in_{n}": a for n, a in arrays.items()}], core_ids=[0])
    return r.results[0]["out"]
```

```python
from contextlib import ExitStack

import concourse.bass as bass
from concourse import mybir

F32 = mybir.dt.float32
BF16 = mybir.dt.bfloat16
I32 = mybir.dt.int32
U32 = mybir.dt.uint32
ALU = mybir.AluOpType
ACT = mybir.ActivationFunctionType
AX = mybir.AxisListType

B, F, D, H, DENSE = 2048, 24, 16, 64, 16
T1, T2 = 512, 256
TB = 128
TILES = B // TB
PAIRS = 2 * TILES
PB = TB // 2
COLS = PB * D
BLK = COLS // 2
BB = BLK // D
CH = COLS // 128
CB = 128 // D
PARTS = 3
KX = PARTS * F
SH = 15
SHC = 5
ONE = SHC * F
FC = F // 2
GF = FC + 1
HG, FG = 16, 8
HGS, FGS = H // HG, F // FG
GP = 4

FIRST = [("one", 2), ("one", 0), ("one", 1)]
LAST = [("two", h, f) for h in range(HGS) for f in range(FGS)]
FULL = FIRST + LAST
PER_SLOT = len(FULL)
SPREADS = 2
X2_AT, GRAM_AT, TURN_AT, SPREAD_AT, GROUP_AT = 1, 3, 6, 9, 12
REST_AT, LO_AT, SUM_AT = 3, 5, 8
NZ = 5
PICKS = [2 * ONE, F, 128]


class Slot:

    def __init__(self, q, r, number=None):
        self.q, self.r = q, r
        self.number = n = number
        self.one = n is None or n < PAIRS
        self.two = n is None or 1 <= n <= PAIRS
        self.gram = n is None or 2 <= n
        self.steps = FULL if self.one and self.two else FIRST if self.one else LAST if self.two else []
        self.turn = r % 2 == 1 and (n is None or n <= PAIRS - 3)
        self.group_ends = self.gram and (r - 2) % GP == GP - 1
        self.done = 0 if n == 0 else q * PER_SLOT - len(LAST)
        self.spreads_done = 0 if n == 0 else q * SPREADS

    def nth(self, pos):
        return self.done + (pos + 1)

    def of(self, kind):
        return [p for p, step in enumerate(self.steps) if step[0] == kind]

    def buffer(self, pos):
        return (pos + (len(FIRST) if self.number != 0 else 0)) % NZ


assert PER_SLOT % NZ == 0


def tower(nc, x):
    with ExitStack() as ctx:
        def sb(name, shape, dt=F32):
            return ctx.enter_context(nc.sbuf_tensor(name, shape, dt))

        def sem(name):
            return ctx.enter_context(nc.semaphore(name))

        w0a = sb("w0a", [ONE, 3, H])
        w0b = sb("w0b", [ONE, 2, H])
        unlike = sb("unlike", [ONE, 1])
        w1 = sb("w1", [128, FC, H])
        w2 = sb("w2", [128, FC, H])
        wt1a = sb("wt1a", [2 * H, T1])
        wt1b = sb("wt1b", [H + DENSE, T1])
        wt2 = sb("wt2", [128, T1 // 128, T2])
        wt3 = sb("wt3", [128, T2 // 128])
        bt1 = sb("bt1", [128, T1 // 128])
        bt2 = sb("bt2", [128, T2 // 128])
        picks = sb("picks", [128, sum(PICKS)], BF16)
        at = [sum(PICKS[:n]) for n in range(len(PICKS) + 1)]
        spread_one = picks[0:KX, at[0]:at[1]].rearrange("k (c m) -> k c m", c=2)
        collect = picks[0:KX, at[1]:at[2]]
        ident = picks[:, at[2]:at[3]]
        ident_f32 = sb("ident_f32", [128, 128])
        own_row = sb("own_row", [128, CB])
        idx = sb("idx", [128, 2, F], I32)
        emb = sb("emb", [TB, 2, F, D])
        rest = sb("rest", [TB, F, D])
        parts = sb("parts", [TB, D, PARTS, F], BF16)
        x0s = sb("x0s", [KX, 2, TB * D], BF16)
        rep = sb("rep", [ONE, 2, COLS])
        ahead = sb("ahead", [ONE, 2, COLS])
        prod = sb("prod", [128, NZ, 2, BLK])
        x1 = sb("x1", [128, BLK])
        x2 = sb("x2", [128, BLK])
        x2t = sb("x2t", [128, CH // 2, 2, H])
        x0t = sb("x0t", [128, 2, CH, F])
        diag = sb("diag", [128, 2, CH, CB, 1 + F])
        sum1 = sb("sum1", [128, PAIRS * BB])
        gram = sb("gram", [128, GF, GP * PB])
        x0w = sb("x0w", [128, 2, FGS, COLS])
        x1w = sb("x1w", [128, HGS, COLS])
        z12 = sb("z12", [2 * H, B])
        z0d = sb("z0d", [H + DENSE, B])
        h1 = [x1w[:, 2 * n:2 * n + 2, :].rearrange("p a c -> p (a c)") for n in range(2)]
        h2 = [sb(f"h2{n}", [128, 2 * 512])[:, :] for n in range(2)] + [prod[:, n].rearrange("p b c -> p (b c)") for n in range(2)]
        y = sb("y", [128, 512])

        ps = [ctx.enter_context(nc.psum_tensor(f"spread{i}", [128, 2, BLK], F32)) for i in range(2)]
        acc1 = ctx.enter_context(nc.psum_tensor("acc1", [128, BLK], F32))
        acc2 = ctx.enter_context(nc.psum_tensor("acc2", [128, BLK], F32))
        misc = [ctx.enter_context(nc.psum_tensor(f"misc{i}", [128, BLK], F32)) for i in range(2)]

        weights_in = sem("weights_in")
        ids_in = [sem(f"ids_in{i}") for i in range(2)]
        gathered = [sem(f"gathered{i}") for i in range(2)]
        stored = sem("stored")
        w0_summed = sem("w0_summed")
        diag_ones, picks_done = sem("diag_ones"), sem("picks_done")
        hi_done, rest_done, mid_done, lo_done = sem("hi_done"), sem("rest_done"), sem("mid_done"), sem("lo_done")
        turned, turn_copied = sem("turned"), sem("turn_copied")
        rep_in = [sem(f"rep_in{i}") for i in range(2)]
        spread = sem("spread")
        multiplied = sem("multiplied")
        contracted = sem("contracted")
        x1_summed, x1_copied, x2_copied = sem("x1_summed"), sem("x1_copied"), sem("x2_copied")
        x0t_ready, x0t_copied = sem("x0t_ready"), sem("x0t_copied")
        diag_done = sem("diag_done")
        x2t_ready, x2t_copied = sem("x2t_ready"), sem("x2t_copied")
        gram_ready, gram_copied = sem("gram_ready"), sem("gram_copied")
        out2_ready, z12_copied, z0_copied = sem("out2_ready"), sem("z12_copied"), sem("z0_copied")
        x0_stored = sem("x0_stored")
        x0w_in = [sem(f"x0w_in{i}") for i in range(2)]
        x1_stored = sem("x1_stored")
        x1w_in = [sem(f"x1w_in{i}") for i in range(HGS)]
        mm1_ready, h1_done = sem("mm1_ready"), sem("h1_done")
        mm2_ready, h2_done = sem("mm2_ready"), sem("h2_done")
        mm3_ready, y_done = sem("mm3_ready"), sem("y_done")

        picks_f32 = prod[:].rearrange("p a b c -> p (a b c)")[:, 0:sum(PICKS)]
        loads = [
            (picks_f32, x["picks"]), (ident_f32[:, :], x["picks"][:, -128:]), (own_row[:, :], x["own_row"]),
        ]
        loads += [(w0a[:, :, :], x["w0_upper"].rearrange("(c p) o -> p c o", p=ONE)),
                  (w0b[:, :, :], x["w0_lower"].rearrange("(c p) o -> p c o", p=ONE)), (unlike[:, :], x["unlike"])]
        loads += [(w1[:, :, :], x["w1"].rearrange("(c p) o -> p c o", p=128))]
        loads += [(w2[:, :, :], x["w2"].rearrange("(c p) o -> p c o", p=128))]
        loads += [(wt1a[:, :], x["wt1"][H:3 * H, :]), (wt1b[0:H, :], x["wt1"][0:H, :]),
                  (wt1b[H:H + DENSE, :], x["wt1"][3 * H:3 * H + DENSE, :]),
                  (z0d[H:H + DENSE, :], x["dense_t"]), (wt2[:, :, :], x["wt2"].rearrange("(c p) n -> p c n", p=128)),
                  (wt3[:, :], x["wt3"]), (bt1[:, :], x["bt1"]), (bt2[:, :], x["bt2"])]
        ALL_LOADED = 16 * len(loads)

        def gathers_of(tile):
            return 16 * F * (tile // 2 + 1)

        def x0w_loads(p):
            return 16 * FGS * (p // 2 + 1)

        def rep_loads(p):
            return 16 * 2 * (p // 2 + 1)

        block = ctx.enter_context(nc.Block())

        @block.sync
        def _(sp):
            def fetch_ids(s, tile, before):
                sp.wait_ge(gathered[s], before)
                sp.dma_start(idx[:, s, :], x["ids"][bass.ds(tile * TB, TB), :]).then_inc(ids_in[s], 16)

            def store_x0(s, tile, gathered_value):
                sp.wait_ge(gathered[s], gathered_value)
                for first, fields in ((0, F), (F, SH - 1)):
                    rows = x["x0_rows"][first:first + fields].rearrange("f (b d) -> b f d", d=D)
                    sp.dma_start(rows[bass.ds(tile * TB, TB)], emb[:, s, 0:fields]).then_inc(x0_stored, 16)
                sp.wait_ge(x0_stored, tile * 32 + 32)

            def load_rep(p, parity):
                cols = bass.ds(p * COLS, COLS)
                src = x["x0_rows"][0:F, cols].unsqueeze(1).broadcast_to([F, SHC, COLS])
                sp.dma_start(rep[:, parity, :], src).then_inc(rep_in[parity], 16)
                src = x["x0_windows"][2 * SHC:2 * SHC + F, :, cols]
                sp.dma_start(ahead[:, parity, :], src).then_inc(rep_in[parity], 16)

            def load_x0w(p, parity):
                for g in range(FGS):
                    src = x["x0_rows"][g * FG:(g + 1) * FG, bass.ds(p * COLS, COLS)]
                    sp.dma_start(x0w[:, parity, g, :], src.unsqueeze(0).broadcast_to([HG, FG, COLS])).then_inc(x0w_in[parity], 16)

            def load_x1w(q, parity, number=None):
                sp.wait_ge(x1_stored, q * 32 + 32)
                for h in range(HGS):
                    if number != 0 and h > 0:
                        sp.wait_ge(multiplied, q * PER_SLOT - len(LAST) + (len(FIRST) + FGS * (h + 1)))
                    rows = x["x1_rows"][parity, HG * h:HG * (h + 1), :]
                    sp.dma_start(x1w[:, h, :], rows.unsqueeze(1).broadcast_to([HG, FG, COLS])).then_inc(x1w_in[h], 16)

            for t in range(2):
                sp.dma_start(idx[:, t, :], x["ids"][t * TB:(t + 1) * TB, :]).then_inc(ids_in[t], 16)
            for dst, src in loads:
                sp.dma_start(dst, src).then_inc(weights_in, 16)
            store_x0(0, 0, gathers_of(0))
            load_rep(0, 0)
            fetch_ids(0, 2, gathers_of(0))
            load_rep(1, 1)
            load_x0w(0, 0)
            load_x1w(0, 0, 0)
            load_x0w(1, 1)
            store_x0(1, 1, gathers_of(1))
            sp.wait_ge(multiplied, 3)
            load_rep(2, 0)
            fetch_ids(1, 3, gathers_of(1))
            load_x1w(1, 1, 1)

            def slot_loads(p, r, tile, gathered_value, ids, last):
                sp.wait_ge(multiplied, p * PER_SLOT - len(LAST))
                load_x0w(p, r % 2)
                if tile is not None:
                    s = (r // 2 + 1) % 2
                    store_x0(s, tile, gathered_value)
                if not last:
                    load_rep(p + 1, (r + 1) % 2)
                if ids:
                    fetch_ids(s, tile + 2, gathered_value)
                load_x1w(p, r % 2)

            with sp.Fori(0, (PAIRS - 8) // 4) as i:
                for j in range(4):
                    odd = j % 2 == 1
                    slot_loads(i * 4 + (2 + j), (2 + j) % 4, i * 2 + (3 + j) // 2 if odd else None,
                               i * (16 * F) + 16 * F * ((3 + j) // 4 + 1), odd, False)
            for p in range(PAIRS - 6, PAIRS):
                tile = (p + 1) // 2 if p % 2 and p < PAIRS - 1 else None
                slot_loads(p, p % 4, tile, gathers_of(tile) if tile else None, False, p == PAIRS - 1)
            sp.wait_ge(y_done, 1)
            sp.dma_start(x["out"].rearrange("(n b) a -> n (b a)", n=4), y[0:128:32, :]).then_inc(stored, 16)
            sp.wait_ge(stored, 16)

        @block.gpsimd
        def _(pool):
            def gather(s, first, last):
                for f in range(first, last):
                    nc.gpsimd.indirect_dma_start(
                        out=emb[:, s, f, :], out_offset=None, in_=x["tables"][f],
                        in_offset=bass.IndirectOffsetOnAxis(ap=idx[:, s, f:f + 1].bitcast(U32), axis=0),
                    ).then_inc(gathered[s], 16)

            def diagonals(slot):
                q, s = slot.q, (slot.r - 1) % 2
                pool.wait_ge(x0t_copied, q)
                if slot.gram:
                    pool.wait_ge(gram_ready, q * 2 - 3)
                nc.gpsimd.tensor_tensor(
                    diag[:, s, :, :, 1:1 + F], x0t[:, s, :, :].unsqueeze(2).broadcast_to([128, CH, CB, F]),
                    own_row[:, :].unsqueeze(1).unsqueeze(3).broadcast_to([128, CH, CB, F]), ALU.mult,
                ).then_inc(diag_done, 1)

            for s in range(2):
                pool.wait_ge(ids_in[s], 16)
                gather(s, 0, F)
            pool.wait_ge(weights_in, ALL_LOADED)
            for s in range(2):
                nc.gpsimd.tensor_copy(diag[:, s, :, :, 0],
                                      own_row[:, :].unsqueeze(1).broadcast_to([128, CH, CB])).then_inc(diag_ones, 1)

            def slot_work(slot, fetch):
                s, half = slot.r // 2, slot.r % 2
                if fetch and half == 0:
                    if slot.number is None:
                        ids_value, rest_value = fetch
                    else:
                        t = slot.q // 2
                        ids_value, rest_value = 16 * ((t + 2) // 2 + 1), t + 1
                    pool.wait_ge(ids_in[s], ids_value)
                    pool.wait_ge(rest_done, rest_value)
                    pool.wait_ge(x0_stored, rest_value * 32)
                if slot.two:
                    diagonals(slot)
                if fetch:
                    gather(s, half * F // 2, (half + 1) * F // 2)

            slot_work(Slot(0, 0, 0), True)
            slot_work(Slot(1, 1, 1), True)
            with pool.Fori(0, (PAIRS - 8) // 4) as i:
                for j in range(4):
                    t0 = 1 + j // 2
                    slot_work(Slot(i * 4 + (2 + j), (2 + j) % 4),
                              (i * 16 + 16 * ((t0 + 2) // 2 + 1), i * 2 + (t0 + 1)))
            for n in range(PAIRS - 6, PAIRS + 1):
                slot_work(Slot(n, n % 4, n), n < PAIRS - 4)

        @block.scalar
        def _(act):
            copy = ACT.Copy

            def split_hi(s, gathered_value, turned_value):
                act.wait_ge(gathered[s], gathered_value)
                if turned_value is not None:
                    act.wait_ge(turned, turned_value)
                nc.scalar.activation(parts[:, :, 0, :].rearrange("p d f -> p f d"), emb[:, s, :, :], copy)\
                    .then_inc(hi_done, 1)

            def split_mid(rest_value):
                act.wait_ge(rest_done, rest_value)
                nc.scalar.activation(parts[:, :, 1, :].rearrange("p d f -> p f d"), rest[:, :, :], copy)\
                    .then_inc(mid_done, 1)

            def copy_turned(s, g, value):
                act.wait_ge(turned, value)
                nc.scalar.activation(
                    x0s[:, s, :].rearrange("k (b d) -> k d b", d=D)[:, g * 8:g * 8 + 8, :],
                    misc[g][0:KX, :].bitcast(BF16).rearrange("k (d b) -> k d b", b=TB), copy,
                ).then_inc(turn_copied, 1)

            def copy_x1(slot):
                act.wait_ge(contracted, slot.nth(slot.of("one")[-1]))
                if slot.number != 0:
                    act.wait_ge(x1_summed, slot.q)
                    act.wait_ge(x1_stored, slot.q * 32)
                nc.scalar.activation(x1[:, :], acc1[:, :], copy).then_inc(x1_copied, 1)

            def store_x1(slot):
                act.wait_ge(x1_copied, slot.q + 1)
                if slot.number != 0:
                    act.wait_ge(multiplied, slot.done + (len(FIRST) + FGS))
                for blk in range(2):
                    act.dma_start(x["x1_rows"][slot.r % 2, :, blk * BLK:(blk + 1) * BLK], x1[H * blk:H * blk + H, :])\
                       .then_inc(x1_stored, 16)

            def copy_x2(slot):
                act.wait_ge(contracted, slot.nth(slot.of("two")[-1]))
                nc.scalar.activation(x2[:, :], acc2[:, :], copy).then_inc(x2_copied, 1)

            def copy_gram(slot, part):
                q = slot.q
                act.wait_ge(gram_ready, q * 2 + (part - 3))
                cols = CH // 2 * CB
                first = (slot.r - 2) % GP * PB + part * cols
                nc.scalar.activation(
                    gram[:, :, first:first + cols].rearrange("p f (c b) -> p c b f", b=CB),
                    misc[part][:, 0:cols * GF].rearrange("p (c b f) -> p c b f", b=CB, f=GF), copy,
                ).then_inc(gram_copied, 1)

            def copy_sum1():
                z0 = z0d[0:H, :].rearrange("p (q k b) -> p k q b", k=2, b=BB)
                for k in range(2):
                    last = nc.scalar.activation(z0[:, k], sum1[H * k:H * k + H, :].rearrange("p (q b) -> p q b", b=BB), copy)
                last.then_inc(z0_copied, 1)

            def hidden1(nb):
                for m in range(T1 // 128):
                    n = nb * (T1 // 128) + m
                    act.wait_ge(mm1_ready, n + 1)
                    if m == 0 and nb >= 2:
                        act.wait_ge(mm2_ready, 2 * (nb - 1))
                    nc.scalar.activation(h1[nb % 2][:, m * 512:(m + 1) * 512], ps[n % 2][:, 0, :], ACT.Relu,
                                         bias=bt1[:, m:m + 1]).then_inc(h1_done, 1)

            def copy_out2(g):
                act.wait_ge(out2_ready, g + 1)
                for k in range(2):
                    half = GP * PB // 2
                    nc.scalar.activation(z12[H:2 * H, bass.ds(g * (GP * PB) + k * half, half)],
                                         misc[0][H * k:H * k + H, 0:half], copy)
                nc.scalar.activation(z12[0:H, bass.ds(g * (GP * PB), GP * PB)], gram[0:H, 0, :], copy)\
                    .then_inc(z12_copied, 1)

            def slot_work(slot, gathered_value, group):
                q, r = slot.q, slot.r
                if slot.number is not None:
                    slot.tile = (q + 1) // 2
                if slot.turn:
                    split_hi(((r + 1) // 2) % 2, gathered_value, q + 1)
                if slot.two:
                    act.wait_ge(x0t_ready, q)
                    if slot.number != 1:
                        act.wait_ge(diag_done, q - 1)
                    nc.scalar.activation(x0t[:, (r - 1) % 2, :, :], misc[0][:, 0:CH * F].rearrange("p (c f) -> p c f", f=F),
                                         copy).then_inc(x0t_copied, 1)
                if slot.gram:
                    act.wait_ge(x2t_ready, q - 1)
                    nc.scalar.activation(x2t[:, :, :, :].rearrange("p c k o -> p (c k o)"), misc[1][:, :], copy)\
                        .then_inc(x2t_copied, 1)
                    if not slot.two:
                        hidden1(0)
                if slot.turn:
                    split_mid(slot.tile + 1)
                if slot.one:
                    copy_x1(slot)
                if slot.gram:
                    copy_gram(slot, 0)
                    copy_gram(slot, 1)
                if slot.one:
                    store_x1(slot)
                if slot.turn:
                    copy_turned(((r + 1) // 2) % 2, 0, q + 2)
                    copy_turned(((r + 1) // 2) % 2, 1, q + 3)
                if slot.gram and not slot.two:
                    hidden1(1)
                if slot.group_ends:
                    copy_out2(group)
                if slot.two:
                    copy_x2(slot)

            act.wait_ge(weights_in, ALL_LOADED)
            nc.scalar.activation(picks[:, :], picks_f32, copy).then_inc(picks_done, 1)
            split_hi(0, gathers_of(0), None)
            split_mid(1)
            copy_turned(0, 0, 1)
            copy_turned(0, 1, 2)
            for n in (0, 1):
                slot = Slot(n, n, n)
                slot_work(slot, gathers_of(1), None)
            with act.Fori(0, (PAIRS - 4) // 4) as i:
                for j in range(4):
                    slot = Slot(i * 4 + (2 + j), (2 + j) % 4)
                    slot.tile = i * 2 + (3 + j) // 2
                    slot_work(slot, i * (16 * F) + 16 * F * ((3 + j) // 4 + 1), i)
            for n in range(PAIRS - 2, PAIRS + 2):
                slot = Slot(n, n % 4, n)
                slot_work(slot, None, PAIRS // GP - 1)
                if n == PAIRS:
                    copy_sum1()

            hidden1(2)
            hidden1(3)

        @block.vector
        def _(dve):
            def split_rest(s, hi_value):
                dve.wait_ge(hi_done, hi_value)
                nc.vector.tensor_tensor(rest[:, :, :], emb[:, s, :, :], parts[:, :, 0, :].rearrange("p d f -> p f d"),
                                        ALU.subtract).then_inc(rest_done, 1)

            def split_lo(mid_value):
                dve.wait_ge(mid_done, mid_value)
                nc.vector.tensor_tensor(parts[:, :, 2, :].rearrange("p d f -> p f d"), rest[:, :, :],
                                        parts[:, :, 1, :].rearrange("p d f -> p f d"), ALU.subtract)\
                    .then_inc(lo_done, 1)

            def product(slot, pos, step):
                nth = slot.nth(pos)
                if slot.number is None or nth - NZ > 0:
                    dve.wait_ge(contracted, nth - NZ)
                dst = prod[:, slot.buffer(pos)].rearrange("p a c -> p (a c)")
                if step[0] == "one":
                    if pos == 0:
                        dve.wait_ge(rep_in[slot.r % 2], slot.rep_value)
                    if step[1] == 2:
                        operand = ahead[:, slot.r % 2, :]
                    else:
                        dve.wait_ge(spread, slot.spreads_done + (step[1] + 1))
                        operand = ps[step[1]][0:ONE, :, :].rearrange("p a c -> p (a c)")
                    nc.vector.tensor_tensor(dst[0:ONE], operand, rep[:, slot.r % 2, :], ALU.mult).then_inc(multiplied, 1)
                else:
                    _, h, f = step
                    if h == 0 and f == 0:
                        dve.wait_ge(x0w_in[(slot.r - 1) % 2], slot.x0w_value)
                    if f == 0:
                        dve.wait_ge(x1w_in[h], slot.q * 16)
                    nc.vector.tensor_tensor(dst, x0w[:, (slot.r - 1) % 2, f, :], x1w[:, h, :], ALU.mult)\
                        .then_inc(multiplied, 1)

            def sum_x1(slot):
                dve.wait_ge(x1_copied, slot.q + 1)
                nc.vector.tensor_reduce(sum1[:, bass.ds(slot.q * BB, BB)], x1[:, :].rearrange("p (b d) -> p b d", d=D),
                                        AX.X, ALU.add).then_inc(x1_summed, 1)

            def slot_work(slot):
                for pos, step in enumerate(slot.steps):
                    product(slot, pos, step)
                    if slot.turn and pos == REST_AT:
                        split_rest(((slot.r + 1) // 2) % 2, slot.split_value)
                    if slot.turn and pos == LO_AT:
                        split_lo(slot.split_value)
                    if slot.one and pos == (SUM_AT if slot.two else len(FIRST) - 1):
                        sum_x1(slot)

            dve.wait_ge(weights_in, ALL_LOADED)
            nc.vector.scalar_tensor_tensor(w0a[:, 0, :], w0b[:, 0, :], unlike[:, 0:1], w0a[:, 0, :], ALU.mult, ALU.add)\
                .then_inc(w0_summed, 1)
            nc.vector.tensor_tensor(w0a[:, 1, :], w0a[:, 1, :], w0b[:, 1, :], ALU.add).then_inc(w0_summed, 1)
            split_rest(0, 1)
            split_lo(1)
            for n in (0, 1):
                slot = Slot(n, n, n)
                slot.split_value, slot.x0w_value = 2, x0w_loads(0)
                slot.rep_value = rep_loads(n)
                slot_work(slot)
            with dve.Fori(0, (PAIRS - 4) // 4) as i:
                for j in range(4):
                    slot = Slot(i * 4 + (2 + j), (2 + j) % 4)
                    slot.split_value = i * 2 + ((3 + j) // 2 + 1)
                    slot.x0w_value = i * (2 * x0w_loads(0)) + x0w_loads(1 + j)
                    slot.rep_value = i * (2 * rep_loads(0)) + rep_loads(2 + j)
                    slot_work(slot)
            for n in range(PAIRS - 2, PAIRS + 2):
                slot = Slot(n, n % 4, n)
                slot.x0w_value, slot.rep_value = x0w_loads(n - 1), rep_loads(n)
                slot_work(slot)

            for nb in range(4):
                for m in range(2):
                    dve.wait_ge(mm2_ready, 2 * nb + m + 1)
                    nc.vector.tensor_scalar(h2[nb][:, m * 512:(m + 1) * 512], ps[m][:, 1, :], bt2[:, m:m + 1], 0.0,
                                            ALU.add, ALU.max).then_inc(h2_done, 1)
            dve.wait_ge(mm3_ready, 1)
            nc.vector.tensor_copy(y[:, :], acc1[:, :]).then_inc(y_done, 1)

        @block.tensor
        def _(pe):
            def turn(g, lo_value):
                if g == 0:
                    pe.wait_ge(lo_done, lo_value)
                dst = misc[g][0:KX, :].bitcast(BF16)
                for k in range(8):
                    m = nc.tensor.transpose(dst[:, k * TB:(k + 1) * TB],
                                            parts[:, g * 8 + k, :, :].rearrange("b p f -> b (p f)"), ident[:, :])
                m.then_inc(turned, 1)

            def spread_into(slot, c):
                if c == 0 and slot.r % 2 == 0:
                    pe.wait_ge(turn_copied, slot.q + 2)
                base = (slot.r % 2) * COLS
                for blk in range(2):
                    m = nc.tensor.matmul(ps[c][0:ONE, blk, :], spread_one[:, c, :],
                                         x0s[:, slot.r // 2, base + blk * BLK:base + (blk + 1) * BLK], start=True, stop=True)
                m.then_inc(spread, 1)

            def contract(slot, pos):
                step, z = slot.steps[pos], prod[:, slot.buffer(pos)]
                if step[0] == "one":
                    steps = slot.of("one")
                    if pos == steps[0] and (slot.number is None or slot.number > 0):
                        pe.wait_ge(x1_copied, slot.q)
                    for blk in range(2):
                        m = nc.tensor.matmul(acc1[H * blk:H * blk + H, :], w0a[:, step[1], :], z[0:ONE, blk, :],
                                             start=pos == steps[0], stop=pos == steps[-1])
                    m.then_inc(contracted, 1)
                    return
                steps = slot.of("two")
                if pos == steps[0] and slot.number != 1:
                    pe.wait_ge(x2_copied, slot.q - 1)
                for blk in range(2):
                    m = nc.tensor.matmul(acc2[H * blk:H * blk + H, :], w1[:, step[1] * FGS + step[2], :], z[:, blk, :],
                                         start=pos == steps[0], stop=pos == steps[-1])
                m.then_inc(contracted, 1)

            def gram_before(slot):
                if slot.number is not None and slot.number >= PAIRS:
                    return True
                return slot.r % 2 == 1 and slot.number != 1

            def collect_x0t(slot):
                r = (slot.r - 1) % 4
                if gram_before(slot):
                    pe.wait_ge(gram_copied, slot.q * 2 - 5)
                for c in range(CH):
                    base = (r % 2) * COLS + c * 128
                    m = nc.tensor.matmul(misc[0][:, c * F:(c + 1) * F], x0s[:, r // 2, base:base + 128], collect[:, :],
                                         start=True, stop=True)
                m.then_inc(x0t_ready, 1)

            def turn_x2(slot):
                q = slot.q
                pe.wait_ge(x2_copied, q - 1)
                if gram_before(slot):
                    pe.wait_ge(gram_copied, q * 2 - 4)
                for c in range(CH // 2):
                    m = nc.tensor.transpose(misc[1][:, c * 128:(c + 1) * 128], x2[:, c * 128:(c + 1) * 128], ident_f32[:, :])
                m.then_inc(x2t_ready, 1)

            def gram_of(slot, part):
                q, s = slot.q, slot.r % 2
                if part == 0:
                    pe.wait_ge(x2t_copied, q - 1)
                    pe.wait_ge(diag_done, q - 1)
                    if slot.two:
                        pe.wait_ge(x0t_copied, q)
                    else:
                        pe.wait_ge(gram_copied, q * 2 - 5)
                width = CB * GF
                for c in range(CH // 2):
                    for odd in range(2):
                        ch = part * (CH // 2) + c
                        m = nc.tensor.matmul(misc[part][H * odd:H * odd + H, c * width:(c + 1) * width], x2t[:, c, part, :],
                                             diag[:, s, ch, :, FC * odd:FC * odd + GF], start=True, stop=True)
                m.then_inc(gram_ready, 1)

            def sum_group(slot):
                pe.wait_ge(gram_copied, slot.q * 2 - 2)
                if slot.turn:
                    pe.wait_ge(turn_copied, slot.q + 2)
                half = GP * PB // 2
                for c in range(FC):
                    for k in range(2):
                        m = nc.tensor.matmul(misc[0][H * k:H * k + H, 0:half], w2[:, c, :],
                                             gram[:, 1 + c, k * half:(k + 1) * half], start=c == 0, stop=c == FC - 1)
                m.then_inc(out2_ready, 1)

            def layer1(nb):
                if nb == 0:
                    pe.wait_ge(z0_copied, 1)
                if nb == 3:
                    pe.wait_ge(z12_copied, PAIRS // GP)
                cols = slice(nb * 512, (nb + 1) * 512)
                for m_ in range(4):
                    n = nb * 4 + m_
                    if n >= 2:
                        pe.wait_ge(h1_done, n - 1)
                    nc.tensor.matmul(ps[n % 2][:, 0, :], wt1a[:, m_ * 128:(m_ + 1) * 128], z12[:, cols], start=True, stop=False)
                    nc.tensor.matmul(ps[n % 2][:, 0, :], wt1b[:, m_ * 128:(m_ + 1) * 128], z0d[:, cols], start=False, stop=True)\
                        .then_inc(mm1_ready, 1)

            def slot_work(before, slot, after, lo_value, group=None):
                q, count = slot.q, len(slot.steps)
                for pos in range(count):
                    pe.wait_ge(multiplied, slot.nth(pos))
                    c = pos - (SPREAD_AT if slot.two else 1)
                    if after.one and 0 <= c < SPREADS:
                        spread_into(after, c)
                    if pos > 0:
                        contract(slot, pos - 1)
                    elif before is not None:
                        contract(before, len(before.steps) - 1)
                    if slot.number == 0 and pos == count - 1:
                        contract(slot, pos)
                    if slot.two and pos == 0:
                        collect_x0t(slot)
                    if slot.gram and pos == X2_AT:
                        turn_x2(slot)
                    if slot.gram and pos in (GRAM_AT, GRAM_AT + 1):
                        gram_of(slot, pos - GRAM_AT)
                    if slot.turn and pos in (TURN_AT, TURN_AT + 1):
                        g = pos - TURN_AT
                        if slot.gram:
                            pe.wait_ge(gram_copied, q * 2 + (g - 3))
                        elif g == 0:
                            pe.wait_ge(x0t_copied, q)
                        turn(g, lo_value)
                    if slot.group_ends and pos == GROUP_AT:
                        sum_group(slot)
                    if slot.group_ends and pos == count - 1:
                        pe.wait_ge(z12_copied, group + 1)

            def last_slot(before, slot):
                contract(before, len(before.steps) - 1)
                turn_x2(slot)
                layer1(0)
                gram_of(slot, 0)
                gram_of(slot, 1)
                layer1(1)
                sum_group(slot)

            pe.wait_ge(weights_in, ALL_LOADED)
            pe.wait_ge(picks_done, 1)
            turn(0, 1)
            turn(1, None)
            pe.wait_ge(turn_copied, 2)
            first, second = Slot(0, 0, 0), Slot(1, 1, 1)
            for c in range(SPREADS):
                spread_into(first, c)
            pe.wait_ge(w0_summed, 2)
            slot_work(None, first, second, None)
            slot_work(None, second, Slot(2, 2, 2), 2)
            pe.wait_ge(diag_ones, 2)
            with pe.Fori(0, (PAIRS - 4) // 4) as i:
                for j in range(4):
                    slot_work(*(Slot(i * 4 + m, m % 4) for m in (1 + j, 2 + j, 3 + j)), i * 2 + ((3 + j) // 2 + 1), i)
            for n in range(PAIRS - 2, PAIRS + 1):
                slot_work(*(Slot(m, m % 4, m) for m in (n - 1, n, n + 1)), None, PAIRS // GP - 1)
            last_slot(Slot(PAIRS, PAIRS % 4, PAIRS), Slot(PAIRS + 1, (PAIRS + 1) % 4, PAIRS + 1))

            def layer2(nb):
                pe.wait_ge(h1_done, 4 * nb + 4)
                if nb > 0:
                    pe.wait_ge(h2_done, 2 * nb)
                for m_ in range(2):
                    for k in range(4):
                        m = nc.tensor.matmul(ps[m_][:, 1, :], wt2[:, k, m_ * 128:(m_ + 1) * 128],
                                             h1[nb % 2][:, k * 512:(k + 1) * 512], start=k == 0, stop=k == 3)
                    m.then_inc(mm2_ready, 1)

            for nb in range(4):
                layer2(nb)
                if nb + 2 < 4:
                    layer1(nb + 2)
            pe.wait_ge(h2_done, 8)
            for k in range(2):
                for nb in range(4):
                    m = nc.tensor.matmul(acc1[32 * nb:32 * nb + 32, :], wt3[:, k:k + 1].broadcast_to([128, 32]),
                                         h2[nb][:, k * 512:(k + 1) * 512], start=k == 0, stop=k == 1)
            m.then_inc(mm3_ready, 1)


def selections(np):
    row_f = np.arange(KX) % F
    f, k = np.arange(ONE) // SHC, np.arange(ONE) % SHC
    one = np.stack([row_f[:, None] == (f + k + SHC * c)[None, :] % F for c in range(2)], axis=1)
    order = list(range(0, F, 2)) + list(range(1, F, 2))
    picks = np.zeros((128, sum(PICKS)), np.float32)
    picks[0:KX, 0:-128] = np.concatenate(
        [one.reshape(KX, -1), row_f[:, None] == np.array(order)[None, :]], axis=1)
    picks[:, -128:] = np.eye(128)
    own_row = np.zeros((128, CB), np.float32)
    own_row[:] = np.arange(128)[:, None] // D == np.arange(CB)[None, :]
    return {"picks": picks, "own_row": own_row, "unlike": (k > 0).astype(np.float32)[:, None]}


def unordered_pairs(np):
    c, f, k = np.meshgrid(np.arange(3), np.arange(F), np.arange(SHC), indexing="ij")
    g = (f + k + SHC * c) % F
    return (f * F + g).reshape(-1), (g * F + f)[0:2].reshape(-1)


def kernel(**inputs):
    import numpy as np
    import concourse.bacc as bacc
    from concourse.bass_utils import run_bass_kernel_spmd

    upper, lower = unordered_pairs(np)
    w0 = np.asarray(inputs["L0_rec_W0"])
    w1 = np.asarray(inputs["L0_rec_W1"]).reshape(FGS, FG, HGS, HG, H).transpose(2, 0, 3, 1, 4).reshape(F * H, H)
    arrays = {
        "dense_t": np.ascontiguousarray(np.asarray(inputs["dense_ctx"]).T), "ids": inputs["ids"],
        "w0_upper": np.ascontiguousarray(w0[upper]), "w0_lower": np.ascontiguousarray(w0[lower]),
        "w1": w1, "w2": inputs["L0_rec_W2"], "wt1": inputs["W_top1"], "wt2": inputs["W_top2"],
        "wt3": inputs["W_top3"].reshape(-1, 128).T, "bt1": inputs["b_top1"].reshape(-1, 128).T,
        "bt2": inputs["b_top2"].reshape(-1, 128).T,
    } | {f"table{f}": inputs[f"tbl_{f}"] for f in range(F)}
    arrays = {n: np.ascontiguousarray(a) for n, a in arrays.items()} | selections(np)
    nc = bacc.Bacc("TRN2", target_bir_lowering=False, num_devices=1)
    aps = {n: nc.dram_tensor(f"in_{n}", a.shape, mybir.dt.from_np(a.dtype), kind="ExternalInput").ap()
           for n, a in arrays.items()}
    aps["tables"] = [aps.pop(f"table{f}") for f in range(F)]
    stride = B * D + 1024
    aps["x0_rows"] = rows = nc.dram_tensor("x0_rows", (F + SH - 1, stride), F32, kind="Internal").ap()
    aps["x0_windows"] = bass.AP(rows.tensor, 0, [[stride, F + 2 * SHC], [stride, SHC], [1, B * D]])
    aps["x1_rows"] = nc.dram_tensor("x1_rows", (2, H, COLS), F32, kind="Internal").ap()
    aps["out"] = nc.dram_tensor("out", (B, 1), F32, kind="ExternalOutput").ap()
    tower(nc, aps)
    r = run_bass_kernel_spmd(nc, [{f"in_{n}": a for n, a in arrays.items()}], core_ids=[0])
    return r.results[0]["out"]
```
